# Optimizing a Trainium2 kernel written in Bass

```python
import numpy as np
import jax
import jax.numpy as jnp

def _softmax(x, axis=-1):
    return jax.nn.softmax(x, axis=axis)

def _gelu(x):
    return jax.nn.gelu(x, approximate=True)

def _silu(x):
    return jax.nn.silu(x)

def _sigmoid(x):
    return jax.nn.sigmoid(x)

def _layernorm(x, axis=-1, eps=1e-05):
    m = jnp.mean(x, axis=axis, keepdims=True)
    v = jnp.var(x, axis=axis, keepdims=True)
    return (x - m) / jnp.sqrt(v + eps)

def _scatter_add(tgt, idx, src, axis=0):
    return tgt.at[idx].add(src)

def _segment_sum(src, seg, n):
    return jax.ops.segment_sum(src, seg, n)
kernel_name = 'mk_adaln_d1_jaxref_r4_c55e5d'

def setup_inputs(seed: int=0):
    np.random.seed(seed)
    _w = jnp.asarray

    def _L0_attn_setup():
        import jax, jax.numpy as jnp
        import numpy as np
        B, T = (4, 512)
        D_MODEL = 256
        N_HEADS = 8
        HEAD_DIM = 64
        KV_LRANK = 64

        def _orthogonalize_per_head(w):
            chunks = w.reshape(N_HEADS, HEAD_DIM, D_MODEL)

            def ns(m):
                A = m @ m.T
                Bm = 1.5 * jnp.eye(HEAD_DIM, dtype=m.dtype) - 0.5 * A
                return Bm @ m
            return jax.vmap(ns)(chunks).reshape(w.shape)
        key = jax.random.key(seed)
        ks = jax.random.split(key, 6)

        def lin(k, out_dim, in_dim):
            bound = 1.0 / np.sqrt(in_dim)
            return jax.random.uniform(k, (out_dim, in_dim), jnp.float32, -bound, bound)
        Wq = _orthogonalize_per_head(lin(ks[0], N_HEADS * HEAD_DIM, D_MODEL))
        return {'x': jax.random.normal(ks[1], (B, T, D_MODEL), jnp.float32), 'Wq': Wq, 'Wkv_down': lin(ks[2], KV_LRANK, D_MODEL), 'Wk_up': lin(ks[3], N_HEADS * HEAD_DIM, KV_LRANK), 'Wv_up': lin(ks[4], N_HEADS * HEAD_DIM, KV_LRANK), 'Wo': lin(ks[5], D_MODEL, N_HEADS * HEAD_DIM)}
    _L0_attn_in = _L0_attn_setup()

    def _L0_ffn_setup():
        import jax, jax.numpy as jnp
        import numpy as np
        R = 64
        key = jax.random.key(seed)
        k1, k2, k3 = jax.random.split(key, 3)
        B, S, D_IN, D_OUT = (8, 1024, 256, 256)
        x = jax.random.normal(k1, (B, S, D_IN), dtype=jnp.float32)
        weight = jax.random.normal(k2, (D_OUT, D_IN), dtype=jnp.float32) * (1.0 / np.sqrt(D_IN))
        disha = jax.random.normal(k3, (R, D_OUT), dtype=jnp.float32) * 0.01
        return {'x': x, 'weight': weight, 'disha': disha}
    _L0_ffn_in = _L0_ffn_setup()
    _L0_c = _w((lambda *s: np.random.randn(*s).astype(np.float32) * 0.05)(16, 256))
    _L0_wmod = _w((lambda *s: np.random.randn(*s).astype(np.float32) * 0.05)(256, 6 * 256) * 256 ** (-0.5))
    _d = {'L0_attn_x': _L0_attn_in['x'], 'L0_attn_Wq': _L0_attn_in['Wq'], 'L0_attn_Wkv_down': _L0_attn_in['Wkv_down'], 'L0_attn_Wk_up': _L0_attn_in['Wk_up'], 'L0_attn_Wv_up': _L0_attn_in['Wv_up'], 'L0_attn_Wo': _L0_attn_in['Wo'], 'L0_ffn_weight': _L0_ffn_in['weight'], 'L0_ffn_disha': _L0_ffn_in['disha'], 'L0_c': _L0_c, 'L0_wmod': _L0_wmod}
    _x0 = _d['L0_attn_x']
    _d['L0_attn_x'] = jax.random.normal(jax.random.fold_in(jax.random.key(seed), 1), (16, 1024, 256), dtype=_x0.dtype)
    del _x0
    return _d

def reference(L0_attn_x, L0_attn_Wq, L0_attn_Wkv_down, L0_attn_Wk_up, L0_attn_Wv_up, L0_attn_Wo, L0_ffn_weight, L0_ffn_disha, L0_c, L0_wmod):

    def _L0_attn_ref(x, Wq, Wkv_down, Wk_up, Wv_up, Wo):
        import jax, jax.numpy as jnp
        import numpy as np
        B, T = (4, 512)
        D_MODEL = 256
        N_HEADS = 8
        HEAD_DIM = 64
        KV_LRANK = 64

        def _orthogonalize_per_head(w):
            chunks = w.reshape(N_HEADS, HEAD_DIM, D_MODEL)

            def ns(m):
                A = m @ m.T
                Bm = 1.5 * jnp.eye(HEAD_DIM, dtype=m.dtype) - 0.5 * A
                return Bm @ m
            return jax.vmap(ns)(chunks).reshape(w.shape)
        b, t, _ = x.shape
        q = (x @ Wq.T).reshape(b, t, N_HEADS, HEAD_DIM)
        kv_latent = x @ Wkv_down.T
        k = (kv_latent @ Wk_up.T).reshape(b, t, N_HEADS, HEAD_DIM)
        v = (kv_latent @ Wv_up.T).reshape(b, t, N_HEADS, HEAD_DIM)
        scale = HEAD_DIM ** (-0.5)
        scores = jnp.einsum('bqhd,bkhd->bhqk', q, k) * scale
        attn = jax.nn.softmax(scores, axis=-1)
        out = jnp.einsum('bhqk,bkhd->bqhd', attn, v)
        out = out.reshape(b, t, N_HEADS * HEAD_DIM)
        return out @ Wo.T

    def _L0_ffn_ref(x, weight, disha):
        import jax, jax.numpy as jnp
        import numpy as np
        R = 64
        result = jnp.einsum('bsd,od->bso', x, weight)
        r = disha.shape[0]
        pooled = x.reshape(*x.shape[:-1], x.shape[-1] // r, r).sum(axis=-2)
        return result + pooled @ disha
    x = L0_attn_x
    mod = (_silu(L0_c) @ L0_wmod).reshape(L0_c.shape[0], 6, 1, -1)
    sa, ca, ga, sb, cb, gb = (mod[:, 0], mod[:, 1], mod[:, 2], mod[:, 3], mod[:, 4], mod[:, 5])
    ga = (2 * (ga >= 0) - 1) * jnp.maximum(jnp.abs(ga), 0.25)
    gb = (2 * (gb >= 0) - 1) * jnp.maximum(jnp.abs(gb), 0.25)
    h = _layernorm(x, axis=-1) * (1 + ca) + sa
    x = x + ga * _L0_attn_ref(h, L0_attn_Wq, L0_attn_Wkv_down, L0_attn_Wk_up, L0_attn_Wv_up, L0_attn_Wo)
    h = _layernorm(x, axis=-1) * (1 + cb) + sb
    x = x + gb * _L0_ffn_ref(h, L0_ffn_weight, L0_ffn_disha)
    return x

_drawn_inputs = setup_inputs


def setup_inputs(seed=0):
    import zlib

    import numpy as np

    out = dict(_drawn_inputs(seed))
    spreads = {}
    factors = {'L0_attn_Wq': 8.0,
     'L0_attn_Wkv_down': 8.0,
     'L0_attn_Wk_up': 8.0,
     'L0_attn_Wv_up': 8.0,
     'L0_attn_Wo': 8.0,
     'L0_ffn_weight': 5.997,
     'L0_ffn_disha': 37.496}
    for name, (base, spread) in spreads.items():
        noise = np.random.default_rng([zlib.crc32(name.encode()), seed]).standard_normal(out[name].shape)
        drawn = base * np.exp(spread * noise) if base else spread * noise
        out[name] = jnp.asarray(drawn.astype(out[name].dtype))
    for name, factor in factors.items():
        out[name] = (out[name] * factor).astype(out[name].dtype)
    return out
```

```python
from contextlib import ExitStack

import concourse.bass as bass
from concourse import mybir

P = 128
ALU = mybir.AluOpType
ACT = mybir.ActivationFunctionType
AX_X = mybir.AxisListType.X
F32 = mybir.dt.float32
F32R = mybir.dt.float32r

B, T, D = 16, 1024, 256
H, HD, R = 8, 64, 64
PAIRS = H // 2
HALF = T // 2
NT = T // P
NF = D // P
STEPS = H * NT
SCALE = float(HD) ** -0.5
EPS = 1e-5
GATE_FLOOR = 0.25
CHUNKS = 4
CT = NT // CHUNKS
RING = 4
POOL_ADDS = 5
DVE_ADDS = NT - 1 - POOL_ADDS

MAX_LAG = 30
STATS_STEP, APPLY_STEP = 3, 7


def step_of(kind, i):
    return {
        "norm_t": 13 + i,
        "latent": 16 + 3 * i,
        "values_t": 21 + i,
        "query": NT * (i + 2) + 4,
        "max_row": MAX_LAG + NT * (i + 1),
        "denominator": NT * (i + 1) + 1,
        "out_proj": 23 + NT * i,
        "norm2_t": 28 + NT * i,
        "ffn": 30 + NT * i,
    }[kind]


BANK_A = {"norm_t": (2 * NF, 1), "values_t": (2, 1), "max_row": (H, 1), "norm2_t": (CHUNKS, -1)}
BANK_B = {"denominator": (H, 0), "latent": (2, 1), "query": (2 * PAIRS, 1), "out_proj": (CHUNKS, -1), "ffn": (CHUNKS, -1)}


class Count:

    def __init__(self, i, per, base):
        self.i, self.per, self.base = i, per, base

    def __add__(self, k):
        if isinstance(k, Count):
            return Count(self.i, self.per + k.per, self.base + k.base)
        return Count(self.i, self.per, self.base + k)

    def __sub__(self, k):
        return self + -k

    def __mul__(self, k):
        return Count(self.i, self.per * k, self.base * k)

    __radd__, __rmul__ = __add__, __mul__

    def value(self):
        return self.i * self.per + self.base


def value(n):
    return n.value() if isinstance(n, Count) else n


class Slot:

    def __init__(self, c, par, has_n=True, has_c=True, has_o=True):
        self.c, self.n, self.o = c, c + 1, c - 1
        self.par = par
        self.has_n, self.has_c, self.has_o = has_n, has_c, has_o
        self.lists = [self._pieces(x) for x in (BANK_A, BANK_B)]

    def _batch(self, which):
        return {1: (self.n, self.has_n), 0: (self.c, self.has_c), -1: (self.o, self.has_o)}[which]

    def _pieces(self, bank):
        found = []
        for rank, (kind, (count, which)) in enumerate(bank.items()):
            for i in range(count):
                s = step_of(kind, i)
                w = which
                if s >= STEPS:
                    s, w = s - STEPS, which - 1
                batch, there = self._batch(w)
                if there:
                    found.append((s, rank, kind, i, w))
        return sorted(found)

    def at(self, s):
        return [(kind, i, bank, self._batch(w)[0], w) for bank, pieces in enumerate(self.lists)
                for (t, _, kind, i, w) in pieces if t == s]

    def before(self, bank):
        if isinstance(self.c, int):
            return sum(len(flagged(c).lists[bank]) for c in range(-1, self.c))
        return (self.c - 1) * len(self.lists[bank]) + flagged(1).before(bank)

    def through(self, bank, kind, i):
        names = [(k, j) for (_, _, k, j, _) in self.lists[bank]]
        return self.before(bank) + names.index((kind, i))

    def max_item(self, s):
        if s >= MAX_LAG:
            return (self.n, s - MAX_LAG) if self.has_n else None
        return (self.c, STEPS - MAX_LAG + s) if self.has_c else None


def flagged(c):
    return Slot(c, c % 2, has_n=c + 1 < B, has_c=0 <= c < B, has_o=c > 0)


def run_slots(eng, body):
    body(flagged(-1))
    body(flagged(0))
    with eng.Fori(0, (B - 2) // 2) as i:
        for u in range(2):
            body(Slot(Count(i, 2, 1 + u), (1 + u) % 2))
    body(flagged(B - 1))
    body(flagged(B))


def need(eng, sem, count):
    if isinstance(count, Count):
        assert count.base > 0, "a wait inside the loop is against zero at first"
    if isinstance(count, Count) or count > 0:
        eng.wait_ge(sem, value(count))


def need_alone(eng, sem, count):
    need(eng, sem, count)
    eng.nop(nofuse=True)


def adaln_block(nc, x, wq, wkv_down, wk_up, wv_up, wo, weight, disha, c, wmod, out):
    gates_dram = nc.dram_tensor("gates_scratch", [B, 2 * D], F32, kind="Internal").ap()

    with ExitStack() as ctx:
        def sb(name, shape, dt=F32):
            return ctx.enter_context(nc.sbuf_tensor(name, shape, dt))

        def psum(name, shape):
            return ctx.enter_context(nc.psum_tensor(name, shape, F32))

        def sem(name):
            return ctx.enter_context(nc.semaphore(name))

        ps_score = [psum(f"ps_score{i}", [P, HALF]) for i in range(2)]
        ps_max = psum("ps_max", [P, T])
        ps_mix = [psum(f"ps_mix{i}", [P, HALF]) for i in range(2)]
        ps_side = [psum("ps_side_a", [P, HALF]), psum("ps_side_b", [P, HALF])]
        ps_a, ps_b = ps_side

        ident = sb("ident", [P, P])
        ones_cols = sb("ones_cols", [P, R])
        ones_row = sb("ones_row", [1, T], F32R)
        minus_half = sb("minus_half", [P, NT])
        w_query = sb("w_query", [P, NF, H * R])
        w_latent = sb("w_latent", [P, NF, P])
        w_out = sb("w_out", [P, PAIRS, D])
        w_ffn = sb("w_ffn", [P, NF, D])
        mod_cols = sb("mod_cols", [P, B, 8])

        w_out_gated = sb("w_out_gated", [P, PAIRS, D])
        w_ffn_gated = sb("w_ffn_gated", [P, NF, D])
        gates = sb("gates", [P, 2, D])
        mod1 = sb("mod1", [P, 4])
        mod2 = sb("mod2", [P, 4])
        x_in = sb("x_in", [P, NT, D])
        stats1 = sb("stats1", [P, NT, 6])
        moments1 = sb("moments1", [P, NT, 2])
        rstd1 = sb("rstd1", [P, 3, NT])
        h_t = sb("h_t", [P, NF, T])
        latent_t = sb("latent_t", [P, T])
        key_hi = [sb(f"key_hi{i}", [P, T], F32R) for i in range(2)]
        key_lo = [sb(f"key_lo{i}", [P, T], F32R) for i in range(2)]
        values = [sb(f"values{i}", [P, NT, R]) for i in range(2)]
        query = sb("query", [P, H, T], F32R)
        query_m = sb("query_m", [P, H, T], F32R)
        neg_max = sb("neg_max", [P, STEPS])
        max_row = [sb(f"max_row{i}", [NT, P], F32R) for i in range(2)]
        probs = sb("probs", [P, RING, T])
        prob_sum = [sb(f"prob_sum{i}", [P, T]) for i in range(2)]
        recip = sb("recip", [P, HALF])
        mixed = [sb(f"mixed{i}", [P, PAIRS, T]) for i in range(2)]

        x_res = [sb(f"x_res{i}", [P, CT, D]) for i in range(2)]
        x_mid = [sb(f"x_mid{i}", [P, CT, D]) for i in range(2)]
        stats2 = sb("stats2", [P, CT, 6])
        moments2 = sb("moments2", [P, CT, 2])
        rstd2 = sb("rstd2", [P, 3, CT])
        x_norm2 = sb("x_norm2", [P, CT, D])
        h2_t = sb("h2_t", [P, NF, CT * P])

        stage = [m[:, :, :].rearrange("p a t -> p (a t)") for m in mixed]
        s_wmod = stage[0][:, 0:3072].rearrange("p (k n) -> p k n", k=NF)
        s_wo = stage[0][:, 3072:4096].rearrange("p (k n) -> p k n", k=NF)
        s_wq = stage[1][:, 0:1024].rearrange("p (k n) -> p k n", k=PAIRS)
        s_wk = stage[1][:, 1024:1280].rearrange("p (k n) -> p k n", k=PAIRS)
        s_wv = stage[1][:, 1280:1536].rearrange("p (k n) -> p k n", k=PAIRS)
        s_wkv = stage[1][0:R, 1536:1792]
        s_weight = stage[1][:, 1792:2304].rearrange("p (k n) -> p k n", k=NF)
        s_disha = stage[1][:, 2304:2560]
        s_c = stage[1][:, 2560:2560 + NF * B].rearrange("p (k b) -> p k b", k=NF)
        s_silu = stage[1][:, 2592:2592 + 3 * NF * B].rearrange("p (j k b) -> p j k b", j=3, k=NF)
        s_wo_t = stage[1][:, 2688:3712].rearrange("p (k n) -> p k n", k=PAIRS)
        s_gate = [x_mid[i][0:B, :, :] for i in range(2)]

        wmod_loaded = sem("wmod_loaded")
        qk_loaded = sem("qk_loaded")
        out_weights_loaded = sem("out_weights_loaded")
        c_loaded = sem("c_loaded")
        consts_made = sem("consts_made")
        ident_made = sem("ident_made")
        exp_c_made = sem("exp_c_made")
        silu_steps = sem("silu_steps")
        fold_a = sem("fold_a")
        fold_a_kept = sem("fold_a_kept")
        fold_b = sem("fold_b")
        fold_b_kept = sem("fold_b_kept")
        gate_steps = sem("gate_steps")
        x_loaded = sem("x_loaded")
        x_res_loaded = [sem(f"x_res_loaded{i}") for i in range(2)]
        gates_loaded = sem("gates_loaded")
        key_row_set = sem("key_row_set")
        query_m_copied = sem("query_m_copied")
        max_row_set = sem("max_row_set")
        out_stored = [sem(f"out_stored{i}") for i in range(2)]
        scores_ready = sem("scores_ready")
        exps_done = sem("exps_done")
        max_scores_ready = sem("max_scores_ready")
        maxima_done = sem("maxima_done")
        full = [sem("a_full"), sem("b_full")]
        a_full, b_full = full
        a_drained = sem("a_drained")
        b_drained = sem("b_drained")
        query_hi_done = sem("query_hi_done")
        key_hi_done = sem("key_hi_done")
        pool_adds = sem("pool_adds")
        dve_adds = sem("dve_adds")
        recips_begun = sem("recips_begun")
        head_mixed = sem("head_mixed")
        stats1_steps = sem("stats1_steps")
        rstd1_steps = sem("rstd1_steps")
        x_normed = sem("x_normed")
        mod1_set = sem("mod1_set")
        mod2_set = sem("mod2_set")
        gated = sem("gated")
        mid_done = sem("mid_done")
        stats2_steps = sem("stats2_steps")
        rstd2_steps = sem("rstd2_steps")
        x_normed2 = sem("x_normed2")

        block = ctx.enter_context(nc.Block())

        @block.sync
        def _(sp):
            for k in range(NF):
                sp.dma_start(s_c[:, k, :], c[:, k * P:(k + 1) * P].rearrange("b p -> p b"),
                             allow_slow_non_contiguous=True).then_inc(c_loaded, 16)
            sp.dma_start(s_wq, wq.rearrange("(k p) n -> p k n", p=P)).then_inc(qk_loaded, 16)
            sp.dma_start(s_wk, wk_up.rearrange("(k p) n -> p k n", p=P)).then_inc(qk_loaded, 16)
            sp.dma_start(s_wkv, wkv_down).then_inc(qk_loaded, 16)
            sp.dma_start(s_wo, wo.rearrange("(k p) n -> p k n", p=P)).then_inc(qk_loaded, 16)
            sp.dma_start(s_wmod, wmod.rearrange("(k p) n -> p k n", p=P)).then_inc(wmod_loaded, 16)
            sp.dma_start(s_wv, wv_up.rearrange("(k p) n -> p k n", p=P)).then_inc(out_weights_loaded, 16)
            sp.dma_start(s_weight, weight.rearrange("(k p) n -> p k n", p=P)).then_inc(out_weights_loaded, 16)
            for k in range(2):
                sp.dma_start(s_disha[k * R:(k + 1) * R, :], disha).then_inc(out_weights_loaded, 16)
            x_v = x.rearrange("b (t p) d -> b p t d", p=P)
            out_v = out.rearrange("b (t p) d -> b p t d", p=P)

            def slot(z):
                for s in range(STEPS):
                    if s == 0 and z.has_n:
                        need_alone(sp, a_full, z.before(0))
                        sp.dma_start(x_in[:, :, :], x_v[value(z.n)]).then_inc(x_loaded, 16)
                        if isinstance(z.n, int) and z.n == 0:
                            sp.wait_ge(gate_steps, 5)
                            for g in range(2):
                                sp.dma_start(gates_dram[:, g * D:(g + 1) * D], s_gate[g][:, g, :]).then_inc(out_stored[g], 16)
                            for g in range(2):
                                sp.wait_ge(out_stored[g], 16)
                    if s == 1 and z.has_o:
                        need_alone(sp, b_drained, z.before(1))
                        sp.dma_start(gates[:, :, :].rearrange("p k d -> p (k d)"),
                                     gates_dram[bass.ds(value(z.o), 1), :].partition_broadcast(P)).then_inc(gates_loaded, 16)
                        for g in range(2):
                            sp.dma_start(x_res[g][:, :, :], x_v[value(z.o)][:, g * CT:(g + 1) * CT, :]).then_inc(x_res_loaded[g], 16)
                    for g in range(2, CHUNKS):
                        if z.has_o and s == step_of("out_proj", g - 2) + 2:
                            need_alone(sp, b_drained, z.through(1, "out_proj", g - 2) + 1)
                            sp.dma_start(x_res[g % 2][:, :, :], x_v[value(z.o)][:, g * CT:(g + 1) * CT, :]).then_inc(x_res_loaded[g % 2], 16)
                    if z.has_n and s == step_of("latent", 1) + 2:
                        need_alone(sp, b_drained, z.through(1, "latent", 1) + 1)
                        sp.dma_start(key_lo[1 - z.par][P - 1:P, :].bitcast(F32), ones_row[:, :].bitcast(F32)).then_inc(key_row_set, 16)
                    for p in range(PAIRS):
                        late = p == PAIRS - 1
                        if s == (step_of("query", 2 * p + 1) + 1) % STEPS and (z.has_c if late else z.has_n):
                            need_alone(sp, b_drained, z.through(1, "query", 2 * p + 1) + 1)
                            sp.dma_start(query_m[:, 2 * p:2 * p + 2, :].bitcast(F32), query[:, 2 * p:2 * p + 2, :].bitcast(F32)).then_inc(query_m_copied, 16)
                    for j in range(H):
                        late = step_of("max_row", j) + 1 >= STEPS
                        if s == (step_of("max_row", j) + 1) % STEPS and (z.has_c if late else z.has_n):
                            b = z.c if late else z.n
                            need_alone(sp, a_drained, z.through(0, "max_row", j) + 1)
                            need_alone(sp, query_m_copied, 16 * (PAIRS * b + j // 2 + 1))
                            need_alone(sp, max_row_set, 16 * (H * b + j))
                            sp.dma_start(query_m[P - 1:P, j, :].bitcast(F32),
                                         max_row[j % 2][:, :].bitcast(F32)).then_inc(max_row_set, 16)
                    for g in range(CHUNKS):
                        if z.has_o and s == step_of("ffn", g) + 1:
                            need_alone(sp, b_drained, z.through(1, "ffn", g) + 1)
                            sp.dma_start(out_v[value(z.o)][:, g * CT:(g + 1) * CT, :], x_mid[g % 2][:, :, :]).then_inc(out_stored[g % 2], 16)

            run_slots(sp, slot)
            for g in range(2):
                sp.wait_ge(out_stored[g], 16 * (B * CHUNKS // 2 + 1))

        @block.tensor
        def _(pe):
            pe.wait_ge(consts_made, 3)
            pe.wait_ge(ident_made, 1)
            pe.wait_ge(qk_loaded, 64)
            fold_out = [ps_score[0], ps_score[1], ps_mix[0], ps_mix[1]]
            for f in range(NF):
                for h in range(H):
                    rows = slice((h % 2) * HD, (h % 2) * HD + HD)
                    last = nc.tensor.matmul(fold_out[2 * f + h % 2][:, (h // 2) * R:(h // 2 + 1) * R],
                                            s_wq[rows, h // 2, f * P:(f + 1) * P], s_wk[rows, h // 2, :],
                                            start=True, stop=True)
            for k in range(NF):
                for p in range(PAIRS):
                    nc.tensor.transpose(ps_max[:, k * HALF + p * P:k * HALF + (p + 1) * P],
                                        s_wo[:, k, p * P:(p + 1) * P], ident[:, :])
            for f in range(NF):
                last = nc.tensor.transpose(ps_a[:, f * R:(f + 1) * R], s_wkv[:, f * P:(f + 1) * P], ident[0:R, 0:R])
            last.then_inc(fold_a, 1)
            pe.wait_ge(wmod_loaded, 16)
            pe.wait_ge(silu_steps, 3)
            for j, part in enumerate((2, 5)):
                for k in range(NF):
                    last = nc.tensor.matmul(ps_b[0:B, j * D:(j + 1) * D], s_silu[:, 2, k, :],
                                            s_wmod[:, k, part * D:(part + 1) * D], start=(k == 0), stop=(k == NF - 1))
            last.then_inc(fold_a, 1)
            pe.wait_ge(fold_a_kept, 9)
            pe.wait_ge(out_weights_loaded, 64)
            for h in range(H):
                rows = slice((h % 2) * HD, (h % 2) * HD + HD)
                bank = fold_out[2 * (h % 2) + h // 4]
                p = h // 2
                nc.tensor.matmul(bank[(h % 2) * R:(h % 2) * R + R, (p % 2) * D:(p % 2 + 1) * D],
                                 s_wv[rows, p, :], s_wo_t[rows, p, :], start=True, stop=True)
            for k in range(NF):
                for o in range(NF):
                    nc.tensor.transpose(ps_max[:, k * HALF + o * P:k * HALF + (o + 1) * P],
                                        s_weight[:, o, k * P:(k + 1) * P], ident[:, :])
            for j, part in enumerate((1, 0, 4, 3)):
                for f in range(NF):
                    for k in range(NF):
                        last = nc.tensor.matmul(ps_a[:, (2 * j + f) * B:(2 * j + f + 1) * B],
                                                s_wmod[:, k, part * D + f * P:part * D + (f + 1) * P],
                                                s_silu[:, 2, k, :], start=(k == 0), stop=(k == NF - 1))
            last.then_inc(fold_b, 1)
            pe.wait_ge(fold_b_kept, 10)
            pe.wait_ge(gate_steps, 2)

            def mix(z, s, steps_done):
                h, k = divmod(s, NT)
                par = z.par
                if k == 0:
                    need(pe, head_mixed, 2 * (H * z.c + h - 1))
                for half in range(2):
                    nc.tensor.matmul(ps_mix[h % 2][half * R:half * R + R, :], values[par][:, k, :],
                                     probs[:, s % RING, half * HALF:(half + 1) * HALF],
                                     start=(k == 0), stop=(k == NT - 1))

            def slot(z):
                for s in range(STEPS):
                    h, k = divmod(s, NT)
                    if z.has_c:
                        if k == 0:
                            need(pe, max_row_set, 16 * (H * z.c + h + 1))
                        if s == 0:
                            need(pe, key_row_set, 16 * (z.c + 1))
                        for half in range(2):
                            cols = slice(half * HALF, (half + 1) * HALF)
                            need(pe, exps_done, 2 * (STEPS * z.c + s) - 1 + half)
                            nc.tensor.matmul(ps_score[half][:, :], key_hi[z.par][:, k * P:(k + 1) * P],
                                             query[:, h, cols], start=True, stop=False)
                            nc.tensor.matmul(ps_score[half][:, :], key_lo[z.par][:, k * P:(k + 1) * P],
                                             query_m[:, h, cols], start=False, stop=True).then_inc(scores_ready, 1)
                    if s == 0 and z.has_o:
                        if not z.has_c:
                            need(pe, exps_done, 2 * STEPS * z.c)
                        zo = Slot(z.o, 1 - z.par)
                        mix(zo, STEPS - 1, None)
                    if s > 0 and z.has_c:
                        if s == 1:
                            need(pe, a_drained, values_drained(z))
                        mix(z, s - 1, None)
                    item = z.max_item(s)
                    if item:
                        b, m = item
                        hm, qt = divmod(m, NT)
                        kpar = (1 - z.par) if s >= MAX_LAG else z.par
                        if m % (2 * NT) == 0:
                            need(pe, b_drained, z.through(1, "query", 2 * (hm // 2) + 1) + 1)
                        need(pe, maxima_done, STEPS * b + m)
                        for half in range(2):
                            last = nc.tensor.matmul(ps_max[:, half * HALF:(half + 1) * HALF],
                                                    query[:, hm, qt * P:(qt + 1) * P],
                                                    key_hi[kpar][:, half * HALF:(half + 1) * HALF],
                                                    start=True, stop=True)
                        last.then_inc(max_scores_ready, 1)
                    for kind, i, bank, b, w in z.at(s):
                        count = z.through(bank, kind, i)
                        side = ps_side[bank]
                        if kind == "norm_t":
                            half, f = divmod(i, NF)
                            t0 = half * NT // 2
                            if f == 0:
                                need(pe, x_normed, NT * b + t0 + NT // 2)
                            need(pe, a_drained, count)
                            for t in range(4):
                                last = nc.tensor.transpose(side[:, t * P:(t + 1) * P],
                                                           x_in[:, t0 + t, f * P:(f + 1) * P], ident[:, :])
                        elif kind == "latent":
                            need(pe, a_drained, z.through(0, "norm_t", NF * i + NF - 1) + 1)
                            need(pe, b_drained, count)
                            for f in range(NF):
                                last = nc.tensor.matmul(side[:, :], w_latent[:, f, :], h_t[:, f, i * HALF:(i + 1) * HALF],
                                                        start=(f == 0), stop=(f == NF - 1))
                        elif kind == "values_t":
                            if i == 0:
                                need(pe, key_hi_done, 4 * (b + 1))
                            need(pe, a_drained, count)
                            for t in range(4):
                                last = nc.tensor.transpose(side[:, t * P:(t + 1) * P],
                                                           latent_t[:, (4 * i + t) * P:(4 * i + t + 1) * P], ident[:, :])
                        elif kind == "query":
                            need(pe, b_drained, count)
                            p, half = divmod(i, 2)
                            for f in range(NF):
                                last = nc.tensor.matmul(side[:, :], w_query[:, f, p * P:(p + 1) * P],
                                                        h_t[:, f, half * HALF:(half + 1) * HALF],
                                                        start=(f == 0), stop=(f == NF - 1))
                        elif kind == "max_row":
                            need(pe, maxima_done, STEPS * b + NT * (i + 1))
                            need(pe, a_drained, count)
                            last = nc.tensor.matmul(side[0:NT, 0:P], neg_max[:, NT * i:NT * (i + 1)], ident[:, :],
                                                    start=True, stop=True)
                        elif kind == "denominator":
                            if DVE_ADDS:
                                need(pe, dve_adds, DVE_ADDS * (H * b + i + 1))
                            else:
                                need(pe, pool_adds, POOL_ADDS * (H * b + i + 1))
                            need(pe, b_drained, count)
                            for half in range(2):
                                last = nc.tensor.matmul(side[half * R:half * R + R, :], ones_cols[:, :],
                                                        prob_sum[i % 2][:, half * HALF:(half + 1) * HALF],
                                                        start=True, stop=True)
                        elif kind == "out_proj":
                            if i == 0:
                                need(pe, head_mixed, 2 * H * (b + 1))
                                need(pe, gated, 2 * (b + 1))
                            need(pe, b_drained, count)
                            for j in range(CT):
                                t = CT * i + j
                                for p in range(PAIRS):
                                    last = nc.tensor.matmul(side[:, j * D:(j + 1) * D],
                                                            mixed[1 - z.par][:, p, t * P:(t + 1) * P],
                                                            w_out_gated[:, p, :], start=(p == 0), stop=(p == PAIRS - 1))
                        elif kind == "norm2_t":
                            need(pe, x_normed2, NT * b + CT * (i + 1))
                            need(pe, a_drained, count)
                            for f in range(NF):
                                for j in range(CT):
                                    last = nc.tensor.transpose(side[:, (f * CT + j) * P:(f * CT + j + 1) * P],
                                                               x_norm2[:, j, f * P:(f + 1) * P], ident[:, :])
                        elif kind == "ffn":
                            need(pe, a_drained, z.through(0, "norm2_t", i) + 1)
                            need(pe, b_drained, count)
                            for j in range(CT):
                                for f in range(NF):
                                    last = nc.tensor.matmul(side[:, j * D:(j + 1) * D], h2_t[:, f, j * P:(j + 1) * P],
                                                            w_ffn_gated[:, f, :], start=(f == 0), stop=(f == NF - 1))
                        last.then_inc(full[bank], 1)

            def values_drained(z):
                before = flagged(z.c - 1) if isinstance(z.c, int) else Slot(z.c - 1, 1 - z.par)
                if not isinstance(z.c, int):
                    names = [(kind, i) for (_, _, kind, i, _) in before.lists[0]]
                    return z.before(0) - (len(names) - names.index(("values_t", 1)) - 1)
                return before.through(0, "values_t", 1) + 1

            run_slots(pe, slot)

        @block.scalar
        def _(act):
            act.wait_ge(c_loaded, 32)
            nc.scalar.activation(s_silu[:, 0, :, :], s_c, ACT.Exp, scale=-1.0).then_inc(exp_c_made, 1)

            def slot(z):
                for s in range(STEPS):
                    h, k = divmod(s, NT)
                    if z.has_c:
                        old = s - RING
                        ho, ko = divmod(old, NT)
                        if ko <= POOL_ADDS:
                            need(act, pool_adds, POOL_ADDS * (H * z.c + ho) + max(ko, 1))
                        else:
                            need(act, dve_adds, DVE_ADDS * (H * z.c + ho) + ko - POOL_ADDS)
                        for half in range(2):
                            need(act, scores_ready, 2 * (STEPS * z.c + s) + half + 1)
                            nc.scalar.activation(probs[:, s % RING, half * HALF:(half + 1) * HALF], ps_score[half][:, :],
                                                 ACT.Exp, scale=SCALE).then_inc(exps_done, 1)
                    for kind, i, bank, b, w in z.at(s):
                        count = z.through(bank, kind, i)
                        if kind == "query":
                            need(act, b_full, count + 1)
                            p, half = divmod(i, 2)
                            for j in range(2):
                                nc.scalar.activation(query[0:R, 2 * p + j, half * HALF:(half + 1) * HALF],
                                                     ps_b[j * R:(j + 1) * R, :], ACT.Copy).then_inc(query_hi_done, 1)
                        elif kind == "latent":
                            need(act, b_full, count + 1)
                            cols = slice(i * HALF, (i + 1) * HALF)
                            nc.scalar.activation(key_hi[1 - z.par][:, cols], ps_b[:, :], ACT.Copy).then_inc(key_hi_done, 1)
                            nc.scalar.activation(latent_t[:, cols], ps_b[:, :], ACT.Copy).then_inc(key_hi_done, 1)
                        elif kind == "norm_t":
                            if i == 0:
                                need(act, mod1_set, b + 1)
                            need(act, a_full, count + 1)
                            half, f = divmod(i, NF)
                            nc.scalar.activation(h_t[:, f, half * HALF:(half + 1) * HALF], ps_a[:, :], ACT.Identity,
                                                 scale=mod1[:, f:f + 1], bias=mod1[:, NF + f:NF + f + 1]).then_inc(a_drained, 1)
                        elif kind == "values_t":
                            need(act, a_full, count + 1)
                            nc.scalar.activation(values[1 - z.par][:, 4 * i:4 * i + 4, :],
                                                 ps_a[:, :].rearrange("p (t n) -> p t n", t=4)[:, :, 0:R],
                                                 ACT.Copy).then_inc(a_drained, 1)
                        elif kind == "norm2_t":
                            if i == 0:
                                need(act, mod2_set, b + 1)
                            need(act, a_full, count + 1)
                            for f in range(NF):
                                last = nc.scalar.activation(h2_t[:, f, :], ps_a[:, f * CT * P:(f + 1) * CT * P], ACT.Identity,
                                                            scale=mod2[:, f:f + 1], bias=mod2[:, NF + f:NF + f + 1])
                            last.then_inc(a_drained, 1)
                        elif kind == "max_row":
                            need(act, a_full, count + 1)
                            need(act, max_row_set, 16 * (H * b + i - 1))
                            nc.scalar.activation(max_row[i % 2][:, :], ps_a[0:NT, 0:P], ACT.Copy).then_inc(a_drained, 1)

            run_slots(act, slot)

        @block.gpsimd
        def _(pool):
            nc.gpsimd.memset(ident[:, :], 0.0).then_inc(consts_made, 1)
            pool.wait_ge(consts_made, 1)
            nc.gpsimd.affine_select(out=ident[:, :], in_=ident[:, :], compare_op=ALU.not_equal, fill=1.0, base=0,
                                    pattern=[[-1, P]], channel_multiplier=1).then_inc(ident_made, 1)
            nc.gpsimd.memset(ones_cols[:, :], 1.0).then_inc(consts_made, 1)
            nc.gpsimd.memset(minus_half[:, :], -0.5).then_inc(consts_made, 1)
            nc.gpsimd.memset(ones_row[:, :].bitcast(F32), 1.0).then_inc(consts_made, 1)

            def inverse_root(moments, rstd, steps, count):
                nc.gpsimd.tensor_scalar(rstd[:, 0, :], moments[:, :, 1], EPS, None, ALU.add).then_inc(steps, 1)
                nc.gpsimd.tensor_scalar(rstd[:, 2, :], moments[:, :, 0], -1.0, None, ALU.mult).then_inc(steps, 1)
                need(pool, steps, count + 2)
                n = rstd.shape[2]
                nc.gpsimd.tensor_tensor(out=rstd[:, 1, :], in0=rstd[:, 0, :], in1=minus_half[:, 0:n], op=ALU.pow).then_inc(steps, 1)
                need_alone(pool, steps, count + 3)

            def add_probs(z, s):
                h, k = divmod(s, NT)
                if not 1 <= k <= POOL_ADDS:
                    return
                done = POOL_ADDS * (H * z.c + h) + k - 1
                total = prob_sum[h % 2]
                need(pool, exps_done, 2 * (STEPS * z.c + s + 1))
                if k > 1:
                    need(pool, pool_adds, done)
                before = probs[:, (s - 1) % RING, :] if k == 1 else total[:, :]
                nc.gpsimd.tensor_tensor(out=total[:, :], in0=before, in1=probs[:, s % RING, :], op=ALU.add).then_inc(pool_adds, 1)

            def slot(z):
                for s in range(STEPS):
                    if s == 0 and z.has_o:
                        add_probs(Slot(z.o, 1 - z.par), STEPS - 1)
                    if s > 0 and z.has_c:
                        add_probs(z, s - 1)
                    if s == 0:
                        if z.has_n:
                            need(pool, a_drained, z.before(0))
                            if isinstance(z.n, int) and z.n == 0:
                                pool.wait_ge(fold_b_kept, 10)
                            nc.gpsimd.tensor_copy(mod1[:, :], mod_cols[:, bass.ds(value(z.n), 1), 0:4].rearrange("p b k -> p (b k)")).then_inc(mod1_set, 1)
                        if z.has_o:
                            need(pool, a_drained, z.before(0))
                            nc.gpsimd.tensor_copy(mod2[:, :], mod_cols[:, bass.ds(value(z.o), 1), 4:8].rearrange("p b k -> p (b k)")).then_inc(mod2_set, 1)
                    if s == APPLY_STEP and z.has_n:
                        need_alone(pool, stats1_steps, 2 * NT * (z.n + 1))
                        inverse_root(moments1, rstd1, rstd1_steps, 3 * z.n)
                    if s in (APPLY_STEP, APPLY_STEP + 1) and z.has_n:
                        for t in range((s - APPLY_STEP) * 4, (s - APPLY_STEP) * 4 + 4):
                            nc.gpsimd.tensor_scalar(x_in[:, t, :], x_in[:, t, :], rstd1[:, 2, t:t + 1], rstd1[:, 1, t:t + 1],
                                                    ALU.add, ALU.mult).then_inc(x_normed, 1)
                    if s == 15 and z.has_o:
                        need(pool, gates_loaded, 16 * (z.o + 1))
                        need(pool, b_full, z.before(1))
                        nc.gpsimd.tensor_tensor(out=w_out_gated[:, :, :], in0=w_out[:, :, :],
                                                in1=gates[:, 0:1, :].broadcast_to([P, PAIRS, D]), op=ALU.mult).then_inc(gated, 1)
                        nc.gpsimd.tensor_tensor(out=w_ffn_gated[:, :, :], in0=w_ffn[:, :, :],
                                                in1=gates[:, 1:2, :].broadcast_to([P, NF, D]), op=ALU.mult).then_inc(gated, 1)
                    for g in range(CHUNKS):
                        if z.has_o and s == step_of("out_proj", g) + 2:
                            need_alone(pool, stats2_steps, 2 * (NT * z.o + CT * (g + 1)))
                            inverse_root(moments2, rstd2, rstd2_steps, 3 * (CHUNKS * z.o + g))
                            for j in range(CT):
                                nc.gpsimd.tensor_scalar(x_norm2[:, j, :], x_mid[g % 2][:, j, :], rstd2[:, 2, j:j + 1],
                                                        rstd2[:, 1, j:j + 1], ALU.add, ALU.mult).then_inc(x_normed2, 1)

            run_slots(pool, slot)

        @block.vector
        def _(dve):
            dve.wait_ge(exp_c_made, 1)
            nc.vector.tensor_scalar(s_silu[:, 1, :, :], s_silu[:, 0, :, :], 1.0, None, ALU.add).then_inc(silu_steps, 1)
            dve.wait_ge(silu_steps, 1)
            nc.vector.reciprocal(s_silu[:, 0, :, :], s_silu[:, 1, :, :]).then_inc(silu_steps, 1)
            dve.wait_ge(silu_steps, 2)
            nc.vector.tensor_tensor(s_silu[:, 2, :, :], s_silu[:, 0, :, :], s_c, ALU.mult).then_inc(silu_steps, 1)
            dve.wait_ge(fold_a, 1)
            fold_out = [ps_score[0], ps_score[1], ps_mix[0], ps_mix[1]]
            for f in range(NF):
                for j in range(2):
                    nc.vector.tensor_copy(w_query[:, f, :].rearrange("p (k j n) -> p k j n", k=PAIRS, j=2)[:, :, j, :],
                                          fold_out[2 * f + j][:, 0:PAIRS * R].rearrange("p (k n) -> p k n", k=PAIRS)).then_inc(fold_a_kept, 1)
            for k in range(NF):
                nc.vector.tensor_copy(s_wo_t[:, :, k * P:(k + 1) * P],
                                      ps_max[:, k * HALF:(k + 1) * HALF].rearrange("p (q n) -> p q n", q=PAIRS)).then_inc(fold_a_kept, 1)
            for j in range(2):
                nc.vector.tensor_copy(w_latent[:, :, j * R:(j + 1) * R],
                                      ps_a[:, 0:NF * R].rearrange("p (f n) -> p f n", f=NF)).then_inc(fold_a_kept, 1)
            dve.wait_ge(fold_a, 2)
            sign, size = s_gate[0], s_gate[1]
            raw = ps_b[0:B, :].rearrange("p (j n) -> p j n", j=2)
            nc.vector.tensor_scalar(sign, raw, 0.0, 2.0, ALU.is_ge, ALU.mult).then_inc(fold_a_kept, 1)
            dve.wait_ge(fold_a_kept, 9)
            nc.vector.tensor_scalar(sign, sign, -1.0, None, ALU.add).then_inc(gate_steps, 1)
            dve.wait_ge(gate_steps, 1)
            nc.vector.tensor_tensor(size, raw, sign, ALU.mult).then_inc(gate_steps, 1)
            dve.wait_ge(gate_steps, 2)
            nc.vector.tensor_scalar(size, size, GATE_FLOOR, None, ALU.max).then_inc(gate_steps, 1)
            dve.wait_ge(gate_steps, 3)
            for j in range(2):
                nc.vector.tensor_tensor(s_gate[j][:, j, :], size[:, j, :], sign[:, j, :], ALU.mult).then_inc(gate_steps, 1)
            dve.wait_ge(fold_b, 1)
            for j in range(2):
                for k in range(2):
                    nc.vector.tensor_copy(w_out[j * R:(j + 1) * R, 2 * k:2 * k + 2, :],
                                          fold_out[2 * j + k][j * R:(j + 1) * R, :].rearrange("p (q n) -> p q n", q=2)).then_inc(fold_b_kept, 1)
            for k in range(NF):
                nc.vector.tensor_tensor(w_ffn[:, k, :], ps_max[:, k * HALF:k * HALF + D], s_disha, ALU.add).then_inc(fold_b_kept, 1)
            cols = ps_a[:, 0:8 * B].rearrange("p (j b) -> p b j", b=B)
            for j in range(2):
                nc.vector.tensor_scalar(mod_cols[:, :, 4 * j:4 * j + 4], cols[:, :, 4 * j:4 * j + 4], 0.0, None, ALU.add).then_inc(fold_b_kept, 1)
            dve.wait_ge(fold_b_kept, 8)
            for j in range(2):
                nc.vector.tensor_scalar(mod_cols[:, :, 4 * j:4 * j + 2], mod_cols[:, :, 4 * j:4 * j + 2], 1.0, None, ALU.add).then_inc(fold_b_kept, 1)

            def add_probs(z, s):
                h, k = divmod(s, NT)
                if k <= POOL_ADDS:
                    return
                head = H * z.c + h
                need(dve, exps_done, 2 * (STEPS * z.c + s + 1))
                if k == POOL_ADDS + 1:
                    need(dve, pool_adds, POOL_ADDS * (head + 1))
                else:
                    need(dve, dve_adds, DVE_ADDS * head + k - POOL_ADDS - 1)
                nc.vector.tensor_tensor(prob_sum[h % 2][:, :], prob_sum[h % 2][:, :], probs[:, s % RING, :], ALU.add).then_inc(dve_adds, 1)

            def slot(z):
                for s in range(STEPS):
                    item = z.max_item(s)
                    if item:
                        b, m = item
                        need(dve, max_scores_ready, STEPS * b + m + 1)
                        nc.vector.tensor_reduce(neg_max[:, m:m + 1], ps_max[:, :], AX_X, ALU.max, negate=True).then_inc(maxima_done, 1)
                    if s == 0 and z.has_o:
                        add_probs(Slot(z.o, 1 - z.par), STEPS - 1)
                    if s > 0 and z.has_c:
                        add_probs(z, s - 1)
                    if z.has_n and STATS_STEP <= s < STATS_STEP + 4:
                        if s == STATS_STEP:
                            need(dve, x_loaded, 16 * (z.n + 1))
                        t0 = 2 * (s - STATS_STEP)
                        for t in (t0, t0 + 1):
                            nc.vector.bn_stats(stats1[:, t, :], x_in[:, t, :]).then_inc(stats1_steps, 1)
                        need_alone(dve, stats1_steps, 2 * NT * z.n + 2 * t0 + 2)
                        for t in (t0, t0 + 1):
                            nc.vector.bn_aggr(moments1[:, t, :], stats1[:, t, :]).then_inc(stats1_steps, 1)
                    for lag in range(3):
                        for kind, i, bank, b, w in z.at(s - lag):
                            if kind != "denominator":
                                continue
                            count = z.through(bank, kind, i)
                            if lag < 2:
                                if lag == 0:
                                    need(dve, b_full, count + 1)
                                cols = slice(lag * HALF // 2, (lag + 1) * HALF // 2)
                                done = recips_begun if lag == 0 else b_drained
                                nc.vector.reciprocal(recip[:, cols], ps_b[:, cols]).then_inc(done, 1)
                            else:
                                need(dve, recips_begun, H * b + i + 1)
                                need(dve, b_drained, count + 1)
                                mpar = z.par if w == 0 else 1 - z.par
                                rows = slice((i % 2) * R, (i % 2) * R + R)
                                for half in range(2):
                                    part = slice(half * R, half * R + R)
                                    nc.vector.tensor_tensor(mixed[mpar][rows, i // 2, half * HALF:(half + 1) * HALF],
                                                            ps_mix[i % 2][part, :], recip[part, :], ALU.mult).then_inc(head_mixed, 1)
                    for kind, i, bank, b, w in z.at(s):
                        if bank == 0 or kind == "denominator":
                            continue
                        count = z.through(bank, kind, i)
                        if kind == "query":
                            need(dve, query_hi_done, 4 * PAIRS * b + 2 * (i + 1))
                            p, half = divmod(i, 2)
                            cols = slice(half * HALF, (half + 1) * HALF)
                            for j in range(2):
                                last = nc.vector.tensor_tensor(query[R:P, 2 * p + j, cols], ps_b[j * R:(j + 1) * R, :],
                                                               query[0:R, 2 * p + j, cols].bitcast(F32), ALU.subtract)
                            last.then_inc(b_drained, 1)
                        elif kind == "latent":
                            need(dve, key_hi_done, 4 * b + 2 * (i + 1))
                            cols = slice(i * HALF, (i + 1) * HALF)
                            nc.vector.tensor_tensor(key_lo[1 - z.par][:, cols], ps_b[:, :],
                                                    key_hi[1 - z.par][:, cols].bitcast(F32), ALU.subtract).then_inc(b_drained, 1)
                        elif kind == "out_proj":
                            need(dve, b_full, count + 1)
                            need(dve, x_res_loaded[i % 2], 16 * (2 * b + i // 2 + 1))
                            need(dve, out_stored[i % 2], 16 * (2 * b + i // 2 + 1))
                            nc.vector.tensor_tensor(x_mid[i % 2][:, :, :], ps_b[:, :].rearrange("p (j d) -> p j d", j=CT),
                                                    x_res[i % 2][:, :, :], ALU.add).then_inc(b_drained, 1)
                            need(dve, b_drained, count + 1)
                            for j in range(CT):
                                nc.vector.bn_stats(stats2[:, j, :], x_mid[i % 2][:, j, :]).then_inc(stats2_steps, 1)
                            need_alone(dve, stats2_steps, 2 * (NT * b + CT * i) + CT)
                            for j in range(CT):
                                nc.vector.bn_aggr(moments2[:, j, :], stats2[:, j, :]).then_inc(stats2_steps, 1)
                        elif kind == "ffn":
                            need(dve, b_full, count + 1)
                            nc.vector.tensor_tensor(x_mid[i % 2][:, :, :], ps_b[:, :].rearrange("p (j d) -> p j d", j=CT),
                                                    x_mid[i % 2][:, :, :], ALU.add).then_inc(b_drained, 1)

            run_slots(dve, slot)


_INS = ['L0_attn_x', 'L0_attn_Wq', 'L0_attn_Wkv_down', 'L0_attn_Wk_up', 'L0_attn_Wv_up', 'L0_attn_Wo',
        'L0_ffn_weight', 'L0_ffn_disha', 'L0_c', 'L0_wmod']
_OUTS = [((B, T, D), 'float32')]


def kernel(**inputs):
    import numpy as _np
    import concourse.bacc as _bacc
    from concourse import mybir as _mybir
    from concourse.bass_utils import run_bass_kernel_spmd as _run

    nc = _bacc.Bacc("TRN2", target_bir_lowering=False, num_devices=1)
    arrays, args = {}, []
    for name in _INS:
        a = _np.ascontiguousarray(inputs[name])
        arrays[f"in_{name}_dram"] = a
        args.append(nc.dram_tensor(f"in_{name}_dram", a.shape, _mybir.dt.from_np(a.dtype), kind="ExternalInput").ap())
    for i, (shape, dtype) in enumerate(_OUTS):
        dt = _mybir.dt.from_np(_np.dtype(dtype))
        args.append(nc.dram_tensor(f"out_{i}_dram", shape, dt, kind="ExternalOutput").ap())
    adaln_block(nc, *args)
    r = _run(nc, [arrays], core_ids=[0])
    got = tuple(r.results[0][f"out_{i}_dram"] for i in range(len(_OUTS)))
    return got[0]
```

```python
from contextlib import ExitStack

import concourse.bass as bass
from concourse import mybir

P = 128
ALU = mybir.AluOpType
ACT = mybir.ActivationFunctionType
AX_X = mybir.AxisListType.X
F32 = mybir.dt.float32
F32R = mybir.dt.float32r

B, T, D = 16, 1024, 256
H, HD, R = 8, 64, 64
PAIRS = H // 2
HALF = T // 2
NT = T // P
NF = D // P
STEPS = H * NT
SCALE = float(HD) ** -0.5
EPS = 1e-5
GATE_FLOOR = 0.25
CHUNKS = 4
CT = NT // CHUNKS
RING = 4
ADDS = NT - 1
CUTS = 4

MAX_LAG = 28
STATS_STEPS = (2, 2, 3, 4, 8, 8, 9, 9)
APPLY_STEPS = (6, 10)


def step_of(kind, i):
    return {
        "norm_t": (11, 13, 14, 15)[i % 4],
        "latent": 14 + 2 * i,
        "values_t": 21 + i,
        "query": NT * (i + 2) + 2,
        "max_row": STEPS - 4 + NT * i,
        "denominator": NT * (i + 1) + 2,
        "out_proj": 25 + NT * i,
        "norm2_t": 30 + NT * i,
        "ffn": 32 + NT * i,
    }[kind]


LAST = {
    "out_proj": (8, 9, 12, 15),
    "norm2_t": (10, 13, 16, 18),
    "ffn": (11, 14, 17, 19),
}

BANK_A = {"norm_t": (2 * NF, 1), "values_t": (2, 1), "max_row": (H, 1), "denominator": (H, 0), "norm2_t": (CHUNKS, -1)}
BANK_B = {"latent": (2, 1), "query": (2 * PAIRS, 1), "out_proj": (CHUNKS, -1), "ffn": (CHUNKS, -1)}


class Count:

    def __init__(self, i, per, base):
        self.i, self.per, self.base = i, per, base

    def __add__(self, k):
        if isinstance(k, Count):
            return Count(self.i, self.per + k.per, self.base + k.base)
        return Count(self.i, self.per, self.base + k)

    def __sub__(self, k):
        return self + -k

    def __mul__(self, k):
        return Count(self.i, self.per * k, self.base * k)

    __radd__, __rmul__ = __add__, __mul__

    def value(self):
        return self.i * self.per + self.base


def value(n):
    return n.value() if isinstance(n, Count) else n


class Slot:

    def __init__(self, c, par, has_n=True, has_c=True, has_o=True):
        self.c, self.n, self.o = c, c + 1, c - 1
        self.par = par
        self.has_n, self.has_c, self.has_o = has_n, has_c, has_o
        self.lists = [self._pieces(x) for x in (BANK_A, BANK_B)]

    def _batch(self, which):
        return {1: (self.n, self.has_n), 0: (self.c, self.has_c), -1: (self.o, self.has_o)}[which]

    def step(self, kind, i):
        if kind in LAST and not self.has_c:
            return LAST[kind][i]
        return step_of(kind, i)

    def _pieces(self, bank):
        found = []
        for rank, (kind, (count, which)) in enumerate(bank.items()):
            for i in range(count):
                s = self.step(kind, i)
                w = which
                if s >= STEPS:
                    s, w = s - STEPS, which - 1
                batch, there = self._batch(w)
                if there:
                    found.append((s, rank, kind, i, w))
        return sorted(found)

    def at(self, s):
        return [(kind, i, bank, self._batch(w)[0], w) for bank, pieces in enumerate(self.lists)
                for (t, _, kind, i, w) in pieces if t == s]

    def before(self, bank):
        if isinstance(self.c, int):
            return sum(len(flagged(c).lists[bank]) for c in range(-1, self.c))
        return (self.c - 1) * len(self.lists[bank]) + flagged(1).before(bank)

    def through(self, bank, kind, i):
        names = [(k, j) for (_, _, k, j, _) in self.lists[bank]]
        return self.before(bank) + names.index((kind, i))

    def max_bank(self, m, ps_max, ps_scores):
        return ps_scores if not self.has_c and self.has_n and m % 2 else ps_max

    def max_item(self, s):
        if s >= MAX_LAG:
            return (self.n, s - MAX_LAG) if self.has_n else None
        return (self.c, STEPS - MAX_LAG + s) if self.has_c else None


def flagged(c):
    return Slot(c, c % 2, has_n=c + 1 < B, has_c=0 <= c < B, has_o=c > 0)


def first(z):
    return isinstance(z.n, int) and z.n == 0


def run_slots(eng, body):
    body(flagged(-1))
    body(flagged(0))
    with eng.Fori(0, (B - 2) // 2) as i:
        for u in range(2):
            body(Slot(Count(i, 2, 1 + u), (1 + u) % 2))
    body(flagged(B - 1))
    body(flagged(B))


def need(eng, sem, count):
    if isinstance(count, Count):
        assert count.base > 0, "a wait inside the loop is against zero at first"
    if isinstance(count, Count) or count > 0:
        eng.wait_ge(sem, value(count))


def need_alone(eng, sem, count):
    need(eng, sem, count)
    eng.nop(nofuse=True)


def adaln_block(nc, x, wq, wkv_down, wk_up, wv_up, wo, weight, disha, c, wmod, out):
    gates_dram = nc.dram_tensor("gates_scratch", [B, 2 * D], F32, kind="Internal").ap()

    with ExitStack() as ctx:
        def sb(name, shape, dt=F32):
            return ctx.enter_context(nc.sbuf_tensor(name, shape, dt))

        def psum(name, shape):
            return ctx.enter_context(nc.psum_tensor(name, shape, F32))

        def sem(name):
            return ctx.enter_context(nc.semaphore(name))

        ps_scores = psum("ps_score", [P, T])
        ps_max = psum("ps_max", [P, T])
        ps_mix = [psum(f"ps_mix{i}", [P, HALF]) for i in range(2)]
        ps_side = [psum("ps_side_a", [P, HALF]), psum("ps_side_b", [P, HALF])]
        ps_a, ps_b = ps_side
        ps_score = [ps_scores[:, i * HALF:(i + 1) * HALF] for i in range(2)]

        ident = sb("ident", [P, P])
        ones_cols = sb("ones_cols", [P, R])
        ones_row = sb("ones_row", [NT, P], F32R)
        minus_half = sb("minus_half", [P, NT])
        w_query = sb("w_query", [P, NF, H * R])
        w_latent = sb("w_latent", [P, NF, P])
        w_out = sb("w_out", [P, PAIRS, D])
        w_ffn = sb("w_ffn", [P, NF, D])
        mod_cols = sb("mod_cols", [P, B, 8])

        w_out_gated = sb("w_out_gated", [P, PAIRS, D])
        w_ffn_gated = sb("w_ffn_gated", [P, NF, D])
        gates = sb("gates", [P, 2, D])
        mod1 = sb("mod1", [P, 4])
        mod2 = sb("mod2", [P, 4])
        x_in = sb("x_in", [P, NT, D])
        stats1 = sb("stats1", [P, NT, 6])
        moments1 = sb("moments1", [P, NT, 2])
        rstd1 = sb("rstd1", [P, 3, NT])
        h_t = sb("h_t", [P, NF, T])
        latent_t = x_in[:, 0:NT // 2, :].rearrange("p t d -> p (t d)")
        key_hi = [sb(f"key_hi{i}", [P, T], F32R) for i in range(2)]
        key_lo = [sb(f"key_lo{i}", [P, T], F32R) for i in range(2)]
        values = [sb(f"values{i}", [P, NT, R]) for i in range(2)]
        query = sb("query", [P, H, T], F32R)
        query_m = sb("query_m", [P, 2, T], F32R)
        neg_max = sb("neg_max", [P, STEPS])
        max_row = [sb(f"max_row{i}", [NT, P], F32R) for i in range(2)]
        probs = sb("probs", [P, RING, T])
        prob_sum = [sb(f"prob_sum{i}", [P, T]) for i in range(2)]
        prob_total = sb("prob_total", [P, HALF])
        recip = sb("recip", [P, HALF])
        mixed_raw = sb("mixed_raw", [P, HALF])
        mixed = [sb(f"mixed{i}", [P, PAIRS, T]) for i in range(2)]

        x_res = [sb(f"x_res{i}", [P, CT, D]) for i in range(CHUNKS)]
        x_mid = [sb(f"x_mid{i}", [P, CT, D]) for i in range(CHUNKS)]
        stats2 = [sb(f"stats2_{i}", [P, CT, 6]) for i in range(2)]
        moments2 = [sb(f"moments2_{i}", [P, CT, 2]) for i in range(2)]
        rstd2 = [sb(f"rstd2_{i}", [P, 3, CT]) for i in range(2)]
        x_norm2 = [sb(f"x_norm2_{i}", [P, CT, D]) for i in range(2)]
        h2_t = sb("h2_t", [P, NF, CT * P])

        stage = [m[:, :, :].rearrange("p a t -> p (a t)") for m in mixed]
        s_wmod = stage[0][:, 0:3072].rearrange("p (k n) -> p k n", k=NF)
        s_wo = stage[0][:, 3072:4096].rearrange("p (k n) -> p k n", k=NF)
        s_wq = stage[1][:, 0:1024].rearrange("p (k n) -> p k n", k=PAIRS)
        s_wk = stage[1][:, 1024:1280].rearrange("p (k n) -> p k n", k=PAIRS)
        s_wv = stage[1][:, 1280:1536].rearrange("p (k n) -> p k n", k=PAIRS)
        s_wkv = stage[1][0:R, 1536:1792]
        s_weight = stage[1][:, 1792:2304].rearrange("p (k n) -> p k n", k=NF)
        s_disha = stage[1][:, 2304:2560]
        s_c = stage[1][:, 2560:2560 + NF * B].rearrange("p (k b) -> p k b", k=NF)
        s_silu = stage[1][:, 2592:2592 + 3 * NF * B].rearrange("p (j k b) -> p j k b", j=3, k=NF)
        s_wo_t = stage[1][:, 2688:3712].rearrange("p (k n) -> p k n", k=PAIRS)
        s_gate = [m[0:B, :, :] for m in x_mid]

        wmod_loaded = sem("wmod_loaded")
        qk_loaded = sem("qk_loaded")
        out_weights_loaded = sem("out_weights_loaded")
        c_loaded = sem("c_loaded")
        consts_made = sem("consts_made")
        ident_made = sem("ident_made")
        exp_c_made = sem("exp_c_made")
        silu_steps = sem("silu_steps")
        fold_a = sem("fold_a")
        fold_a_kept = sem("fold_a_kept")
        fold_b = sem("fold_b")
        fold_b_kept = sem("fold_b_kept")
        gate_steps = sem("gate_steps")
        x_loaded = sem("x_loaded")
        x_res_loaded = [sem(f"x_res_loaded{i}") for i in range(CHUNKS)]
        gates_loaded = sem("gates_loaded")
        key_row_set = sem("key_row_set")
        query_m_copied = sem("query_m_copied")
        max_row_set = sem("max_row_set")
        out_stored = [sem(f"out_stored{i}") for i in range(CHUNKS)]
        scores_ready = sem("scores_ready")
        exps_done = sem("exps_done")
        max_scores_ready = sem("max_scores_ready")
        maxima_done = sem("maxima_done")
        full = [sem("a_full"), sem("b_full")]
        a_full, b_full = full
        a_drained = sem("a_drained")
        b_drained = sem("b_drained")
        query_hi_done = sem("query_hi_done")
        key_hi_done = sem("key_hi_done")
        adds_done = sem("adds_done")
        heads_done = sem("heads_done")
        heads_kept = sem("heads_kept")
        recips_done = sem("recips_done")
        head_mixed = sem("head_mixed")
        stats1_steps = sem("stats1_steps")
        rstd1_steps = sem("rstd1_steps")
        x_normed = sem("x_normed")
        mod1_set = sem("mod1_set")
        mod2_set = sem("mod2_set")
        gated = sem("gated")
        mid_done = sem("mid_done")
        stats2_steps = sem("stats2_steps")
        rstd2_steps = sem("rstd2_steps")
        x_normed2 = sem("x_normed2")

        block = ctx.enter_context(nc.Block())

        @block.sync
        def _(sp):
            for k in range(NF):
                sp.dma_start(s_c[:, k, :], c[:, k * P:(k + 1) * P].rearrange("b p -> p b"),
                             allow_slow_non_contiguous=True).then_inc(c_loaded, 16)
            sp.dma_start(s_wq, wq.rearrange("(k p) n -> p k n", p=P)).then_inc(qk_loaded, 16)
            sp.dma_start(s_wk, wk_up.rearrange("(k p) n -> p k n", p=P)).then_inc(qk_loaded, 16)
            sp.dma_start(s_wkv, wkv_down).then_inc(qk_loaded, 16)
            sp.dma_start(s_wo, wo.rearrange("(k p) n -> p k n", p=P)).then_inc(qk_loaded, 16)
            x_v = x.rearrange("b (t p) d -> b p t d", p=P)
            sp.dma_start(x_in[:, :, :], x_v[0]).then_inc(x_loaded, 16)
            sp.dma_start(s_wmod, wmod.rearrange("(k p) n -> p k n", p=P)).then_inc(wmod_loaded, 16)
            sp.dma_start(s_wv, wv_up.rearrange("(k p) n -> p k n", p=P)).then_inc(out_weights_loaded, 16)
            sp.dma_start(s_weight, weight.rearrange("(k p) n -> p k n", p=P)).then_inc(out_weights_loaded, 16)
            for k in range(2):
                sp.dma_start(s_disha[k * R:(k + 1) * R, :], disha).then_inc(out_weights_loaded, 16)
            out_v = out.rearrange("b (t p) d -> b p t d", p=P)

            def slot(z):
                for s in range(STEPS):
                    if s == 0 and z.has_n:
                        if not first(z):
                            need_alone(sp, a_full, z.before(0))
                            sp.dma_start(x_in[:, :, :], x_v[value(z.n)]).then_inc(x_loaded, 16)
                        else:
                            sp.wait_ge(gate_steps, 3 + CHUNKS)
                            for g in range(CHUNKS):
                                j, cols = g // 2, slice(g % 2 * P, (g % 2 + 1) * P)
                                sp.dma_start(gates_dram[:, g * P:(g + 1) * P], s_gate[g][:, j, cols]).then_inc(out_stored[g], 16)
                            for g in range(CHUNKS):
                                sp.wait_ge(out_stored[g], 16)
                    if s == 1 and z.has_o:
                        need_alone(sp, b_drained, z.before(1))
                        sp.dma_start(gates[:, :, :].rearrange("p k d -> p (k d)"),
                                     gates_dram[bass.ds(value(z.o), 1), :].partition_broadcast(P)).then_inc(gates_loaded, 16)
                        for g in range(CHUNKS):
                            sp.dma_start(x_res[g][:, :, :], x_v[value(z.o)][:, g * CT:(g + 1) * CT, :]).then_inc(x_res_loaded[g], 16)
                    if z.has_n and s == step_of("latent", 1) + 2:
                        need_alone(sp, b_drained, z.through(1, "latent", 1) + 1)
                        sp.dma_start(key_lo[1 - z.par][P - 1:P, :].bitcast(F32), ones_row[:, :].bitcast(F32)).then_inc(key_row_set, 16)
                    for j in range(H):
                        copy, row = STEPS + NT * (j - 1) + 1, step_of("max_row", j) + 1
                        late = row >= STEPS
                        b, there = (z.c, z.has_c) if late else (z.n, z.has_n)
                        if s == copy % STEPS and there:
                            need_alone(sp, scores_ready, 2 * NT * (H * b + j - 1))
                            if j == 0:
                                need_alone(sp, b_drained, z.through(1, "query", 1) + 1)
                            elif j == 6:
                                need_alone(sp, b_drained, z.through(1, "query", 7) + 1)
                            elif j in (2, 4):
                                need_alone(sp, b_drained, z.before(1))
                            sp.dma_start(query_m[:, j % 2, :].bitcast(F32), query[:, j, :].bitcast(F32)).then_inc(query_m_copied, 16)
                        if s == row % STEPS and there:
                            need_alone(sp, a_drained, z.through(0, "max_row", j) + 1)
                            need_alone(sp, query_m_copied, 16 * (H * b + j + 1))
                            need_alone(sp, max_row_set, 16 * (H * b + j))
                            sp.dma_start(query_m[P - 1:P, j % 2, :].bitcast(F32),
                                         max_row[j % 2][:, :].bitcast(F32)).then_inc(max_row_set, 16)
                    for g in range(CHUNKS):
                        if z.has_o and s == z.step("ffn", g) + 1:
                            need_alone(sp, b_drained, z.through(1, "ffn", g) + 1)
                            sp.dma_start(out_v[value(z.o)][:, g * CT:(g + 1) * CT, :], x_mid[g][:, :, :]).then_inc(out_stored[g], 16)

            run_slots(sp, slot)
            for g in range(CHUNKS):
                sp.wait_ge(out_stored[g], 16 * (B + 1))

        @block.tensor
        def _(pe):
            pe.wait_ge(consts_made, 3)
            pe.wait_ge(ident_made, 1)
            pe.wait_ge(qk_loaded, 64)
            fold_out = [ps_score[0], ps_score[1], ps_mix[0], ps_mix[1]]
            for f in range(NF):
                for h in range(H):
                    rows = slice((h % 2) * HD, (h % 2) * HD + HD)
                    last = nc.tensor.matmul(fold_out[2 * f + h % 2][:, (h // 2) * R:(h // 2 + 1) * R],
                                            s_wq[rows, h // 2, f * P:(f + 1) * P], s_wk[rows, h // 2, :],
                                            start=True, stop=True)
            for k in range(NF):
                for p in range(PAIRS):
                    nc.tensor.transpose(ps_max[:, k * HALF + p * P:k * HALF + (p + 1) * P],
                                        s_wo[:, k, p * P:(p + 1) * P], ident[:, :])
            for f in range(NF):
                last = nc.tensor.transpose(ps_a[:, f * R:(f + 1) * R], s_wkv[:, f * P:(f + 1) * P], ident[0:R, 0:R])
            last.then_inc(fold_a, 1)
            pe.wait_ge(wmod_loaded, 16)
            pe.wait_ge(silu_steps, 3)
            for j, part in enumerate((2, 5)):
                for k in range(NF):
                    last = nc.tensor.matmul(ps_b[0:B, j * D:(j + 1) * D], s_silu[:, 2, k, :],
                                            s_wmod[:, k, part * D:(part + 1) * D], start=(k == 0), stop=(k == NF - 1))
            last.then_inc(fold_a, 1)
            pe.wait_ge(fold_a_kept, 9)
            pe.wait_ge(out_weights_loaded, 64)
            for h in range(H):
                rows = slice((h % 2) * HD, (h % 2) * HD + HD)
                bank = fold_out[2 * (h % 2) + h // 4]
                p = h // 2
                nc.tensor.matmul(bank[(h % 2) * R:(h % 2) * R + R, (p % 2) * D:(p % 2 + 1) * D],
                                 s_wv[rows, p, :], s_wo_t[rows, p, :], start=True, stop=True)
            for k in range(NF):
                for o in range(NF):
                    nc.tensor.transpose(ps_max[:, k * HALF + o * P:k * HALF + (o + 1) * P],
                                        s_weight[:, o, k * P:(k + 1) * P], ident[:, :])
            for j, part in enumerate((1, 0, 4, 3)):
                for f in range(NF):
                    for k in range(NF):
                        last = nc.tensor.matmul(ps_a[:, (2 * j + f) * B:(2 * j + f + 1) * B],
                                                s_wmod[:, k, part * D + f * P:part * D + (f + 1) * P],
                                                s_silu[:, 2, k, :], start=(k == 0), stop=(k == NF - 1))
            last.then_inc(fold_b, 1)
            pe.wait_ge(fold_b_kept, 10)
            pe.wait_ge(gate_steps, 2)

            def mix(z, s, steps_done):
                h, k = divmod(s, NT)
                par = z.par
                if k == 0:
                    need(pe, heads_kept, H * z.c + h - 1)
                for half in range(2):
                    last = nc.tensor.matmul(ps_mix[h % 2][half * R:half * R + R, :], values[par][:, k, :],
                                     probs[:, s % RING, half * HALF:(half + 1) * HALF],
                                     start=(k == 0), stop=(k == NT - 1))
                if k == NT - 1:
                    last.then_inc(heads_done, 1)

            def slot(z):
                for s in range(STEPS):
                    h, k = divmod(s, NT)
                    if z.has_c:
                        if k == 0:
                            need(pe, max_row_set, 16 * (H * z.c + h + 1))
                        if s == 0:
                            need(pe, key_row_set, 16 * (z.c + 1))
                            if isinstance(z.c, int) and z.c == 0:
                                pe.wait_ge(maxima_done, STEPS - MAX_LAG)
                        for half in range(2):
                            cols = slice(half * HALF, (half + 1) * HALF)
                            need(pe, exps_done, 2 * (STEPS * z.c + s) - 1 + half)
                            nc.tensor.matmul(ps_score[half], key_hi[z.par][:, k * P:(k + 1) * P],
                                             query[:, h, cols], start=True, stop=False)
                            nc.tensor.matmul(ps_score[half], key_lo[z.par][:, k * P:(k + 1) * P],
                                             query_m[:, h % 2, cols], start=False, stop=True).then_inc(scores_ready, 1)
                    if s == 0 and z.has_o:
                        if not z.has_c:
                            need(pe, exps_done, 2 * STEPS * z.c)
                        zo = Slot(z.o, 1 - z.par)
                        mix(zo, STEPS - 1, None)
                    if s > 0 and z.has_c:
                        if s == 1:
                            need(pe, a_drained, values_drained(z))
                        mix(z, s - 1, None)
                    item = z.max_item(s)
                    if item:
                        b, m = item
                        hm, qt = divmod(m, NT)
                        kpar = (1 - z.par) if s >= MAX_LAG else z.par
                        if m % (2 * NT) == 0:
                            need(pe, b_drained, z.through(1, "query", 2 * (hm // 2) + 1) + 1)
                        need(pe, maxima_done, STEPS * b + m - (0 if z.has_c else 1))
                        bank = z.max_bank(m, ps_max, ps_scores)
                        for half in range(2):
                            last = nc.tensor.matmul(bank[:, half * HALF:(half + 1) * HALF],
                                                    query[:, hm, qt * P:(qt + 1) * P],
                                                    key_hi[kpar][:, half * HALF:(half + 1) * HALF],
                                                    start=True, stop=True)
                        last.then_inc(max_scores_ready, 1)
                    for kind, i, bank, b, w in z.at(s):
                        count = z.through(bank, kind, i)
                        side = ps_side[bank]
                        if kind == "norm_t":
                            half, f = divmod(i, NF)
                            t0 = half * NT // 2
                            if f == 0:
                                need(pe, x_normed, NT * b + t0 + NT // 2)
                            need(pe, a_drained, count)
                            for t in range(4):
                                last = nc.tensor.transpose(side[:, t * P:(t + 1) * P],
                                                           x_in[:, t0 + t, f * P:(f + 1) * P], ident[:, :])
                        elif kind == "latent":
                            need(pe, a_drained, z.through(0, "norm_t", NF * i + NF - 1) + 1)
                            need(pe, b_drained, count)
                            for f in range(NF):
                                last = nc.tensor.matmul(side[:, :], w_latent[:, f, :], h_t[:, f, i * HALF:(i + 1) * HALF],
                                                        start=(f == 0), stop=(f == NF - 1))
                        elif kind == "values_t":
                            if i == 0:
                                need(pe, key_hi_done, 4 * (b + 1))
                            need(pe, a_drained, count)
                            for t in range(4):
                                last = nc.tensor.transpose(side[:, t * P:(t + 1) * P],
                                                           latent_t[:, (4 * i + t) * P:(4 * i + t + 1) * P], ident[:, :])
                        elif kind == "query":
                            need(pe, b_drained, count)
                            p, half = divmod(i, 2)
                            for f in range(NF):
                                last = nc.tensor.matmul(side[:, :], w_query[:, f, p * P:(p + 1) * P],
                                                        h_t[:, f, half * HALF:(half + 1) * HALF],
                                                        start=(f == 0), stop=(f == NF - 1))
                        elif kind == "max_row":
                            need(pe, maxima_done, STEPS * b + NT * (i + 1))
                            need(pe, a_drained, count)
                            last = nc.tensor.matmul(side[0:NT, 0:P], neg_max[:, NT * i:NT * (i + 1)], ident[:, :],
                                                    start=True, stop=True)
                        elif kind == "denominator":
                            need(pe, adds_done, ADDS * (H * b + i + 1))
                            need(pe, a_drained, count)
                            for half in range(2):
                                last = nc.tensor.matmul(side[half * R:half * R + R, :], ones_cols[:, :],
                                                        prob_sum[i % 2][:, half * HALF:(half + 1) * HALF],
                                                        start=True, stop=True)
                        elif kind == "out_proj":
                            if i == 0:
                                need(pe, head_mixed, 2 * H * (b + 1))
                                need(pe, gated, 2 * (b + 1))
                            need(pe, b_drained, count)
                            for j in range(CT):
                                t = CT * i + j
                                for p in range(PAIRS):
                                    last = nc.tensor.matmul(side[:, j * D:(j + 1) * D],
                                                            mixed[1 - z.par][:, p, t * P:(t + 1) * P],
                                                            w_out_gated[:, p, :], start=(p == 0), stop=(p == PAIRS - 1))
                        elif kind == "norm2_t":
                            need(pe, x_normed2, NT * b + CT * (i + 1))
                            need(pe, a_drained, count)
                            for f in range(NF):
                                for j in range(CT):
                                    last = nc.tensor.transpose(side[:, (f * CT + j) * P:(f * CT + j + 1) * P],
                                                               x_norm2[i % 2][:, j, f * P:(f + 1) * P], ident[:, :])
                        elif kind == "ffn":
                            need(pe, a_drained, z.through(0, "norm2_t", i) + 1)
                            need(pe, b_drained, count)
                            for j in range(CT):
                                for f in range(NF):
                                    last = nc.tensor.matmul(side[:, j * D:(j + 1) * D], h2_t[:, f, j * P:(j + 1) * P],
                                                            w_ffn_gated[:, f, :], start=(f == 0), stop=(f == NF - 1))
                        last.then_inc(full[bank], 1)

            def values_drained(z):
                before = flagged(z.c - 1) if isinstance(z.c, int) else Slot(z.c - 1, 1 - z.par)
                if not isinstance(z.c, int):
                    names = [(kind, i) for (_, _, kind, i, _) in before.lists[0]]
                    return z.before(0) - (len(names) - names.index(("values_t", 1)) - 1)
                return before.through(0, "values_t", 1) + 1

            run_slots(pe, slot)

        @block.scalar
        def _(act):
            act.wait_ge(c_loaded, 32)
            nc.scalar.activation(s_silu[:, 0, :, :], s_c, ACT.Exp, scale=-1.0).then_inc(exp_c_made, 1)

            def slot(z):
                for s in range(STEPS):
                    h, k = divmod(s, NT)
                    if z.has_c:
                        old = s - RING
                        ho, ko = divmod(old, NT)
                        need(act, adds_done, ADDS * (H * z.c + ho) + max(ko, 1))
                        for half in range(2):
                            need(act, scores_ready, 2 * (STEPS * z.c + s) + half + 1)
                            nc.scalar.activation(probs[:, s % RING, half * HALF:(half + 1) * HALF], ps_score[half],
                                                 ACT.Exp, scale=SCALE).then_inc(exps_done, 1)
                    if k == 0 and (z.has_c if h else z.has_o):
                        head, bank_of = (H * z.c + h - 1, (h - 1) % 2) if h else (H * z.o + H - 1, 1)
                        need(act, heads_done, head + 1)
                        need(act, head_mixed, 2 * head)
                        nc.scalar.activation(mixed_raw[:, :], ps_mix[bank_of][:, :], ACT.Copy).then_inc(heads_kept, 1)
                    for kind, i, bank, b, w in z.at(s):
                        count = z.through(bank, kind, i)
                        if kind == "query":
                            need(act, b_full, count + 1)
                            p, half = divmod(i, 2)
                            for j in range(2):
                                nc.scalar.activation(query[0:R, 2 * p + j, half * HALF:(half + 1) * HALF],
                                                     ps_b[j * R:(j + 1) * R, :], ACT.Copy).then_inc(query_hi_done, 1)
                        elif kind == "latent":
                            need(act, b_full, count + 1)
                            cols = slice(i * HALF, (i + 1) * HALF)
                            nc.scalar.activation(key_hi[1 - z.par][:, cols], ps_b[:, :], ACT.Copy).then_inc(key_hi_done, 1)
                            nc.scalar.activation(latent_t[:, cols], ps_b[:, :], ACT.Copy).then_inc(key_hi_done, 1)
                        elif kind == "norm_t":
                            if i == 0:
                                need(act, mod1_set, b + 1)
                            need(act, a_full, count + 1)
                            half, f = divmod(i, NF)
                            nc.scalar.activation(h_t[:, f, half * HALF:(half + 1) * HALF], ps_a[:, :], ACT.Identity,
                                                 scale=mod1[:, f:f + 1], bias=mod1[:, NF + f:NF + f + 1]).then_inc(a_drained, 1)
                        elif kind == "values_t":
                            need(act, a_full, count + 1)
                            nc.scalar.activation(values[1 - z.par][:, 4 * i:4 * i + 4, :],
                                                 ps_a[:, :].rearrange("p (t n) -> p t n", t=4)[:, :, 0:R],
                                                 ACT.Copy).then_inc(a_drained, 1)
                        elif kind == "denominator":
                            need(act, a_full, count + 1)
                            need(act, recips_done, CUTS * (H * b + i))
                            nc.scalar.activation(prob_total[:, :], ps_a[:, :], ACT.Copy).then_inc(a_drained, 1)
                        elif kind == "norm2_t":
                            if i == 0:
                                need(act, mod2_set, b + 1)
                            need(act, a_full, count + 1)
                            for f in range(NF):
                                last = nc.scalar.activation(h2_t[:, f, :], ps_a[:, f * CT * P:(f + 1) * CT * P], ACT.Identity,
                                                            scale=mod2[:, f:f + 1], bias=mod2[:, NF + f:NF + f + 1])
                            last.then_inc(a_drained, 1)
                        elif kind == "max_row":
                            need(act, a_full, count + 1)
                            need(act, max_row_set, 16 * (H * b + i - 1))
                            nc.scalar.activation(max_row[i % 2][:, :], ps_a[0:NT, 0:P], ACT.Copy).then_inc(a_drained, 1)

            run_slots(act, slot)

        @block.gpsimd
        def _(pool):
            nc.gpsimd.memset(ident[:, :], 0.0).then_inc(consts_made, 1)
            pool.wait_ge(consts_made, 1)
            nc.gpsimd.affine_select(out=ident[:, :], in_=ident[:, :], compare_op=ALU.not_equal, fill=1.0, base=0,
                                    pattern=[[-1, P]], channel_multiplier=1).then_inc(ident_made, 1)
            nc.gpsimd.memset(ones_cols[:, :], 1.0).then_inc(consts_made, 1)
            nc.gpsimd.memset(minus_half[:, :], -0.5).then_inc(consts_made, 1)
            nc.gpsimd.memset(ones_row[:, :].bitcast(F32), 1.0).then_inc(consts_made, 1)

            def inverse_root(moments, rstd, steps, count):
                nc.gpsimd.tensor_scalar(rstd[:, 0, :], moments[:, :, 1], EPS, None, ALU.add).then_inc(steps, 1)
                nc.gpsimd.tensor_scalar(rstd[:, 2, :], moments[:, :, 0], -1.0, None, ALU.mult).then_inc(steps, 1)
                need(pool, steps, count + 2)
                n = rstd.shape[2]
                nc.gpsimd.tensor_tensor(out=rstd[:, 1, :], in0=rstd[:, 0, :], in1=minus_half[:, 0:n], op=ALU.pow).then_inc(steps, 1)
                need_alone(pool, steps, count + 3)

            def add_probs(z, s):
                h, k = divmod(s, NT)
                if k == 0:
                    return
                done = ADDS * (H * z.c + h) + k - 1
                total = prob_sum[h % 2]
                need(pool, exps_done, 2 * (STEPS * z.c + s + 1))
                if k > 1:
                    need(pool, adds_done, done)
                before = probs[:, (s - 1) % RING, :] if k == 1 else total[:, :]
                nc.gpsimd.tensor_tensor(out=total[:, :], in0=before, in1=probs[:, s % RING, :], op=ALU.add).then_inc(adds_done, 1)

            def slot(z):
                for s in range(STEPS):
                    if s == 0 and z.has_o:
                        add_probs(Slot(z.o, 1 - z.par), STEPS - 1)
                    if s > 0 and z.has_c:
                        add_probs(z, s - 1)
                    if s == 0:
                        if z.has_o:
                            need(pool, a_drained, z.before(0))
                            nc.gpsimd.tensor_copy(mod2[:, :], mod_cols[:, bass.ds(value(z.o), 1), 4:8].rearrange("p b k -> p (b k)")).then_inc(mod2_set, 1)
                    if s in APPLY_STEPS and z.has_n:
                        half = APPLY_STEPS.index(s)
                        tiles = slice(half * NT // 2, (half + 1) * NT // 2)
                        need_alone(pool, stats1_steps, 2 * NT * z.n + NT * (half + 1))
                        inverse_root(moments1[:, tiles, :], rstd1[:, :, tiles], rstd1_steps, 3 * (2 * z.n + half))
                        for t in range(NT)[tiles]:
                            nc.gpsimd.tensor_scalar(x_in[:, t, :], x_in[:, t, :], rstd1[:, 2, t:t + 1], rstd1[:, 1, t:t + 1],
                                                    ALU.add, ALU.mult).then_inc(x_normed, 1)
                    if s == APPLY_STEPS[-1] and z.has_n:
                        need(pool, a_drained, z.before(0))
                        if first(z):
                            pool.wait_ge(fold_b_kept, 10)
                        nc.gpsimd.tensor_copy(mod1[:, :], mod_cols[:, bass.ds(value(z.n), 1), 0:4].rearrange("p b k -> p (b k)")).then_inc(mod1_set, 1)
                    if s == (15 if z.has_c else 1) and z.has_o:
                        need(pool, gates_loaded, 16 * (z.o + 1))
                        need(pool, b_full, z.before(1))
                        nc.gpsimd.tensor_tensor(out=w_out_gated[:, :, :], in0=w_out[:, :, :],
                                                in1=gates[:, 0:1, :].broadcast_to([P, PAIRS, D]), op=ALU.mult).then_inc(gated, 1)
                        nc.gpsimd.tensor_tensor(out=w_ffn_gated[:, :, :], in0=w_ffn[:, :, :],
                                                in1=gates[:, 1:2, :].broadcast_to([P, NF, D]), op=ALU.mult).then_inc(gated, 1)
                    for g in range(CHUNKS):
                        if z.has_o and s == z.step("out_proj", g) + 2:
                            need_alone(pool, stats2_steps, 2 * (NT * z.o + CT * (g + 1)))
                            inverse_root(moments2[g % 2], rstd2[g % 2], rstd2_steps, 3 * (CHUNKS * z.o + g))
                            for j in range(CT):
                                nc.gpsimd.tensor_scalar(x_norm2[g % 2][:, j, :], x_mid[g][:, j, :], rstd2[g % 2][:, 2, j:j + 1],
                                                        rstd2[g % 2][:, 1, j:j + 1], ALU.add, ALU.mult).then_inc(x_normed2, 1)

            run_slots(pool, slot)

        @block.vector
        def _(dve):
            def statistics(n, t):
                if t == 0:
                    need(dve, x_loaded, 16 * (n + 1))
                nc.vector.bn_stats(stats1[:, t, :], x_in[:, t, :]).then_inc(stats1_steps, 1)
                need_alone(dve, stats1_steps, 2 * (NT * n + t) + 1)
                nc.vector.bn_aggr(moments1[:, t, :], stats1[:, t, :]).then_inc(stats1_steps, 1)

            dve.wait_ge(exp_c_made, 1)
            nc.vector.tensor_scalar(s_silu[:, 1, :, :], s_silu[:, 0, :, :], 1.0, None, ALU.add).then_inc(silu_steps, 1)
            dve.wait_ge(silu_steps, 1)
            nc.vector.reciprocal(s_silu[:, 0, :, :], s_silu[:, 1, :, :]).then_inc(silu_steps, 1)
            dve.wait_ge(silu_steps, 2)
            nc.vector.tensor_tensor(s_silu[:, 2, :, :], s_silu[:, 0, :, :], s_c, ALU.mult).then_inc(silu_steps, 1)
            for t in range(NT):
                statistics(0, t)
            dve.wait_ge(fold_a, 1)
            fold_out = [ps_score[0], ps_score[1], ps_mix[0], ps_mix[1]]
            for f in range(NF):
                for j in range(2):
                    nc.vector.tensor_copy(w_query[:, f, :].rearrange("p (k j n) -> p k j n", k=PAIRS, j=2)[:, :, j, :],
                                          fold_out[2 * f + j][:, 0:PAIRS * R].rearrange("p (k n) -> p k n", k=PAIRS)).then_inc(fold_a_kept, 1)
            for k in range(NF):
                nc.vector.tensor_copy(s_wo_t[:, :, k * P:(k + 1) * P],
                                      ps_max[:, k * HALF:(k + 1) * HALF].rearrange("p (q n) -> p q n", q=PAIRS)).then_inc(fold_a_kept, 1)
            for j in range(2):
                nc.vector.tensor_copy(w_latent[:, :, j * R:(j + 1) * R],
                                      ps_a[:, 0:NF * R].rearrange("p (f n) -> p f n", f=NF)).then_inc(fold_a_kept, 1)
            dve.wait_ge(fold_a, 2)
            sign, size = s_gate[0], s_gate[1]
            raw = ps_b[0:B, :].rearrange("p (j n) -> p j n", j=2)
            nc.vector.tensor_scalar(sign, raw, 0.0, 2.0, ALU.is_ge, ALU.mult).then_inc(fold_a_kept, 1)
            dve.wait_ge(fold_a_kept, 9)
            nc.vector.tensor_scalar(sign, sign, -1.0, None, ALU.add).then_inc(gate_steps, 1)
            dve.wait_ge(gate_steps, 1)
            nc.vector.tensor_tensor(size, raw, sign, ALU.mult).then_inc(gate_steps, 1)
            dve.wait_ge(gate_steps, 2)
            nc.vector.tensor_scalar(size, size, GATE_FLOOR, None, ALU.max).then_inc(gate_steps, 1)
            dve.wait_ge(gate_steps, 3)
            for g in range(CHUNKS):
                j, cols = g // 2, slice(g % 2 * P, (g % 2 + 1) * P)
                nc.vector.tensor_tensor(s_gate[g][:, j, cols], size[:, j, cols], sign[:, j, cols], ALU.mult).then_inc(gate_steps, 1)
            dve.wait_ge(fold_b, 1)
            for j in range(2):
                for k in range(2):
                    nc.vector.tensor_copy(w_out[j * R:(j + 1) * R, 2 * k:2 * k + 2, :],
                                          fold_out[2 * j + k][j * R:(j + 1) * R, :].rearrange("p (q n) -> p q n", q=2)).then_inc(fold_b_kept, 1)
            for k in range(NF):
                nc.vector.tensor_tensor(w_ffn[:, k, :], ps_max[:, k * HALF:k * HALF + D], s_disha, ALU.add).then_inc(fold_b_kept, 1)
            cols = ps_a[:, 0:8 * B].rearrange("p (j b) -> p b j", b=B)
            for j in range(2):
                nc.vector.tensor_scalar(mod_cols[:, :, 4 * j:4 * j + 4], cols[:, :, 4 * j:4 * j + 4], 0.0, None, ALU.add).then_inc(fold_b_kept, 1)
            dve.wait_ge(fold_b_kept, 8)
            for j in range(2):
                nc.vector.tensor_scalar(mod_cols[:, :, 4 * j:4 * j + 2], mod_cols[:, :, 4 * j:4 * j + 2], 1.0, None, ALU.add).then_inc(fold_b_kept, 1)

            def divide(z, s):
                for lag in range(1, CUTS + 2):
                    for kind, i, bank, b, w in z.at(s - lag):
                        if kind != "denominator":
                            continue
                        if lag <= CUTS:
                            if lag == 1:
                                need(dve, a_drained, z.through(bank, kind, i) + 1)
                            cols = slice((lag - 1) * HALF // CUTS, lag * HALF // CUTS)
                            nc.vector.reciprocal(recip[:, cols], prob_total[:, cols]).then_inc(recips_done, 1)
                            continue
                        need(dve, recips_done, CUTS * (H * b + i + 1))
                        need(dve, heads_kept, H * b + i + 1)
                        mpar = z.par if w == 0 else 1 - z.par
                        rows = slice((i % 2) * R, (i % 2) * R + R)
                        for half in range(2):
                            part = slice(half * R, half * R + R)
                            nc.vector.tensor_tensor(mixed[mpar][rows, i // 2, half * HALF:(half + 1) * HALF],
                                                    mixed_raw[part, :], recip[part, :], ALU.mult).then_inc(head_mixed, 1)

            def slot(z):
                for s in range(STEPS):
                    item = z.max_item(s)
                    if item:
                        b, m = item
                        need(dve, max_scores_ready, STEPS * b + m + 1)
                        nc.vector.tensor_reduce(neg_max[:, m:m + 1], z.max_bank(m, ps_max, ps_scores)[:, :], AX_X, ALU.max, negate=True).then_inc(maxima_done, 1)
                    divide(z, s)
                    for t in range(NT):
                        if z.has_n and not first(z) and s == STATS_STEPS[t]:
                            statistics(z.n, t)
                    for kind, i, bank, b, w in z.at(s):
                        if bank == 0:
                            continue
                        count = z.through(bank, kind, i)
                        if kind == "query":
                            need(dve, query_hi_done, 4 * PAIRS * b + 2 * (i + 1))
                            p, half = divmod(i, 2)
                            cols = slice(half * HALF, (half + 1) * HALF)
                            for j in range(2):
                                last = nc.vector.tensor_tensor(query[R:P, 2 * p + j, cols], ps_b[j * R:(j + 1) * R, :],
                                                               query[0:R, 2 * p + j, cols].bitcast(F32), ALU.subtract)
                            last.then_inc(b_drained, 1)
                        elif kind == "latent":
                            need(dve, key_hi_done, 4 * b + 2 * (i + 1))
                            cols = slice(i * HALF, (i + 1) * HALF)
                            nc.vector.tensor_tensor(key_lo[1 - z.par][:, cols], ps_b[:, :],
                                                    key_hi[1 - z.par][:, cols].bitcast(F32), ALU.subtract).then_inc(b_drained, 1)
                        elif kind == "out_proj":
                            need(dve, b_full, count + 1)
                            need(dve, x_res_loaded[i], 16 * (b + 1))
                            need(dve, out_stored[i], 16 * (b + 1))
                            nc.vector.tensor_tensor(x_mid[i][:, :, :], ps_b[:, :].rearrange("p (j d) -> p j d", j=CT),
                                                    x_res[i][:, :, :], ALU.add).then_inc(b_drained, 1)
                            need(dve, b_drained, count + 1)
                            for j in range(CT):
                                nc.vector.bn_stats(stats2[i % 2][:, j, :], x_mid[i][:, j, :]).then_inc(stats2_steps, 1)
                            need_alone(dve, stats2_steps, 2 * (NT * b + CT * i) + CT)
                            for j in range(CT):
                                nc.vector.bn_aggr(moments2[i % 2][:, j, :], stats2[i % 2][:, j, :]).then_inc(stats2_steps, 1)
                        elif kind == "ffn":
                            need(dve, b_full, count + 1)
                            nc.vector.tensor_tensor(x_mid[i][:, :, :], ps_b[:, :].rearrange("p (j d) -> p j d", j=CT),
                                                    x_mid[i][:, :, :], ALU.add).then_inc(b_drained, 1)

            run_slots(dve, slot)


_INS = ['L0_attn_x', 'L0_attn_Wq', 'L0_attn_Wkv_down', 'L0_attn_Wk_up', 'L0_attn_Wv_up', 'L0_attn_Wo',
        'L0_ffn_weight', 'L0_ffn_disha', 'L0_c', 'L0_wmod']
_OUTS = [((B, T, D), 'float32')]


def kernel(**inputs):
    import numpy as _np
    import concourse.bacc as _bacc
    from concourse import mybir as _mybir
    from concourse.bass_utils import run_bass_kernel_spmd as _run

    nc = _bacc.Bacc("TRN2", target_bir_lowering=False, num_devices=1)
    arrays, args = {}, []
    for name in _INS:
        a = _np.ascontiguousarray(inputs[name])
        arrays[f"in_{name}_dram"] = a
        args.append(nc.dram_tensor(f"in_{name}_dram", a.shape, _mybir.dt.from_np(a.dtype), kind="ExternalInput").ap())
    for i, (shape, dtype) in enumerate(_OUTS):
        dt = _mybir.dt.from_np(_np.dtype(dtype))
        args.append(nc.dram_tensor(f"out_{i}_dram", shape, dt, kind="ExternalOutput").ap())
    adaln_block(nc, *args)
    r = _run(nc, [arrays], core_ids=[0])
    got = tuple(r.results[0][f"out_{i}_dram"] for i in range(len(_OUTS)))
    return got[0]
```

```python
from contextlib import ExitStack

import concourse.bass as bass
from concourse import mybir

P = 128
ALU = mybir.AluOpType
ACT = mybir.ActivationFunctionType
AX_X = mybir.AxisListType.X
F32 = mybir.dt.float32
F32R = mybir.dt.float32r

B, T, D = 16, 1024, 256
H, HD, R = 8, 64, 64
PAIRS = H // 2
HALF = T // 2
NT = T // P
NF = D // P
STEPS = H * NT
SCALE = float(HD) ** -0.5
EPS = 1e-5
GATE_FLOOR = 0.25
CHUNKS = 4
CT = NT // CHUNKS
RING = 4
ADDS = NT - 1
CUTS = 2
QUARTERS = 4
QW, QP = T // QUARTERS, P // QUARTERS
MIX_LAGS = (3, 4)

MAX_LAG = 48
STATS_STEPS = (2, 2, 3, 4, 8, 8, 9, 9)
APPLY_STEPS = (6, 10)

GATE_STEPS = ((1, 13), (3, 16), (7, 17))


def step_of(kind, i):
    return {
        "norm_t": (11, 13, 14, 15)[i % 4],
        "latent": 15 + 2 * i,
        "values_t": 21 + i,
        "query": NT * (i + 2) + 2,
        "max_row": STEPS - 4 + NT * i,
        "denominator": NT * (i + 1) + 2,
        "mixed_hi": 18 + NT * i,
        "mixed_lo": 18 + NT * i,
        "out_proj": 25 + NT * i,
        "norm2_t": 30 + NT * i,
        "h2_split": 31 + NT * i,
        "ffn": 32 + NT * i,
    }[kind]


LAST = {
    "mixed_hi": (8, 8, 9, 10),
    "mixed_lo": (8, 8, 10, 11),
    "out_proj": (8, 9, 11, 14),
    "norm2_t": (10, 13, 16, 18),
    "h2_split": (11, 14, 16, 18),
    "ffn": (12, 15, 17, 19),
}

BANK_A = {"norm_t": (2 * NF, 1), "values_t": (2, 1), "max_row": (H, 1), "denominator": (H, 0), "norm2_t": (CHUNKS, -1)}
BANK_B = {"latent": (2, 1), "query": (2 * PAIRS, 1), "out_proj": (CHUNKS, -1), "ffn": (CHUNKS, -1)}


class Count:

    def __init__(self, i, per, base):
        self.i, self.per, self.base = i, per, base

    def __add__(self, k):
        if isinstance(k, Count):
            return Count(self.i, self.per + k.per, self.base + k.base)
        return Count(self.i, self.per, self.base + k)

    def __sub__(self, k):
        return self + -k

    def __mul__(self, k):
        return Count(self.i, self.per * k, self.base * k)

    __radd__, __rmul__ = __add__, __mul__

    def value(self):
        return self.i * self.per + self.base


def value(n):
    return n.value() if isinstance(n, Count) else n


class Slot:

    def __init__(self, c, par, has_n=True, has_c=True, has_o=True):
        self.c, self.n, self.o = c, c + 1, c - 1
        self.par = par
        self.has_n, self.has_c, self.has_o = has_n, has_c, has_o
        self.lists = [self._pieces(x) for x in (BANK_A, BANK_B)]

    def _batch(self, which):
        return {1: (self.n, self.has_n), 0: (self.c, self.has_c), -1: (self.o, self.has_o)}[which]

    def step(self, kind, i):
        if kind in LAST and not self.has_c:
            return LAST[kind][i]
        return step_of(kind, i)

    def _pieces(self, bank):
        found = []
        for rank, (kind, (count, which)) in enumerate(bank.items()):
            for i in range(count):
                s = self.step(kind, i)
                w = which
                if s >= STEPS:
                    s, w = s - STEPS, which - 1
                batch, there = self._batch(w)
                if there:
                    found.append((s, rank, kind, i, w))
        return sorted(found)

    def at(self, s):
        return [(kind, i, bank, self._batch(w)[0], w) for bank, pieces in enumerate(self.lists)
                for (t, _, kind, i, w) in pieces if t == s]

    def before(self, bank):
        if isinstance(self.c, int):
            return sum(len(flagged(c).lists[bank]) for c in range(-1, self.c))
        return (self.c - 1) * len(self.lists[bank]) + flagged(1).before(bank)

    def through(self, bank, kind, i):
        names = [(k, j) for (_, _, k, j, _) in self.lists[bank]]
        return self.before(bank) + names.index((kind, i))

    def max_bank(self, m, ps_max, ps_scores):
        return ps_scores if not self.has_c and self.has_n and m % 2 else ps_max

    def max_item(self, s):
        if s >= MAX_LAG:
            return (self.n, s - MAX_LAG) if self.has_n else None
        return (self.c, STEPS - MAX_LAG + s) if self.has_c else None


def flagged(c):
    return Slot(c, c % 2, has_n=c + 1 < B, has_c=0 <= c < B, has_o=c > 0)


def first(z):
    return isinstance(z.n, int) and z.n == 0


def run_slots(eng, body):
    body(flagged(-1))
    body(flagged(0))
    with eng.Fori(0, (B - 2) // 2) as i:
        for u in range(2):
            body(Slot(Count(i, 2, 1 + u), (1 + u) % 2))
    body(flagged(B - 1))
    body(flagged(B))


def need(eng, sem, count):
    if isinstance(count, Count):
        assert count.base > 0, "a wait inside the loop is against zero at first"
    if isinstance(count, Count) or count > 0:
        eng.wait_ge(sem, value(count))


def need_alone(eng, sem, count):
    need(eng, sem, count)
    eng.nop(nofuse=True)


def adaln_block(nc, x, wq, wkv_down, wk_up, wv_up, wo, weight, disha, c, wmod, out):
    gates_dram = nc.dram_tensor("gates_scratch", [B, 2 * D], F32, kind="Internal").ap()

    with ExitStack() as ctx:
        def sb(name, shape, dt=F32):
            return ctx.enter_context(nc.sbuf_tensor(name, shape, dt))

        def psum(name, shape):
            return ctx.enter_context(nc.psum_tensor(name, shape, F32))

        def sem(name):
            return ctx.enter_context(nc.semaphore(name))

        ps_scores = psum("ps_score", [P, T])
        ps_max = psum("ps_max", [P, T])
        ps_mix = [psum(f"ps_mix{i}", [P, HALF]) for i in range(2)]
        ps_side = [psum("ps_side_a", [P, HALF]), psum("ps_side_b", [P, HALF])]
        ps_a, ps_b = ps_side
        ps_score = [ps_scores[:, i * HALF:(i + 1) * HALF] for i in range(2)]

        ident = sb("ident", [P, P])
        ones_cols = sb("ones_cols", [P, QP])
        ones_row = sb("ones_row", [NT, P], F32R)
        minus_half = sb("minus_half", [P, NT])
        w_in_hi = sb("w_in_hi", [P, NF, H * R + P], F32R)
        w_in_lo = sb("w_in_lo", [P, NF, H * R + P], F32R)
        w_out = sb("w_out", [P, PAIRS, D])
        w_ffn = sb("w_ffn", [P, NF, D])
        mod_cols = sb("mod_cols", [P, B, 8])

        w_out_gated = sb("w_out_gated", [P, PAIRS, D])
        w_out_hi = sb("w_out_hi", [P, PAIRS, D], F32R)
        w_out_lo = sb("w_out_lo", [P, PAIRS, D], F32R)
        w_ffn_hi = sb("w_ffn_hi", [P, NF, D], F32R)
        w_ffn_lo = sb("w_ffn_lo", [P, NF, D], F32R)
        mod1 = sb("mod1", [P, 4])
        mod2 = sb("mod2", [P, 4])
        x_in = sb("x_in", [P, NT, D])
        stats1 = sb("stats1", [P, NT, 6])
        moments1 = sb("moments1", [P, NT, 2])
        rstd1 = sb("rstd1", [P, 3, NT])
        h_hi = sb("h_hi", [P, NF, T], F32R)
        h_lo = sb("h_lo", [P, NF, T], F32R)
        h_whole = sb("h_whole", [P, 2, HALF])
        latent_t = x_in[:, 0:NT // 2, :].rearrange("p t d -> p (t d)")
        key_hi = [sb(f"key_hi{i}", [P, T], F32R) for i in range(2)]
        key_lo = [sb(f"key_lo{i}", [P, T], F32R) for i in range(2)]
        values = [sb(f"values{i}", [P, NT, R]) for i in range(2)]
        query = sb("query", [P, H, T], F32R)
        query_m = sb("query_m", [P, 2, T], F32R)
        neg_max = sb("neg_max", [P, STEPS])
        max_row = [sb(f"max_row{i}", [NT, P], F32R) for i in range(2)]
        probs = sb("probs", [P, RING, T])
        prob_sum = [sb(f"prob_sum{i}", [P, T]) for i in range(2)]
        recip = sb("recip", [P, QW])
        prob_total = recip
        mixed_raw = sb("mixed_raw", [P, HALF])
        mixed = [sb(f"mixed{i}", [P, PAIRS, T]) for i in range(2)]

        mixed_hi = sb("mixed_hi", [P, PAIRS, CT * P], F32R)
        mixed_lo = sb("mixed_lo", [P, PAIRS, CT * P], F32R)
        x_mid = [sb(f"x_mid{i}", [P, CT, D]) for i in range(CHUNKS)]
        stats2 = [sb(f"stats2_{i}", [P, CT, 6]) for i in range(2)]
        moments2 = [sb(f"moments2_{i}", [P, CT, 2]) for i in range(2)]
        rstd2 = [sb(f"rstd2_{i}", [P, 3, CT]) for i in range(2)]
        x_norm2 = sb("x_norm2", [P, CT, D])
        h2_t = sb("h2_t", [P, NF, CT * P])
        h2_hi = sb("h2_hi", [P, NF, CT * P], F32R)
        h2_lo = sb("h2_lo", [P, NF, CT * P], F32R)
        gates = h2_t[:, :, :]
        w_ffn_gated = x_norm2[:, :, :]

        stage = [m[:, :, :].rearrange("p a t -> p (a t)") for m in mixed]
        s_wmod = stage[0][:, 0:3072].rearrange("p (k n) -> p k n", k=NF)
        s_wo = stage[0][:, 3072:4096].rearrange("p (k n) -> p k n", k=NF)
        s_wq = stage[1][:, 0:1024].rearrange("p (k n) -> p k n", k=PAIRS)
        s_wk = stage[1][:, 1024:1280].rearrange("p (k n) -> p k n", k=PAIRS)
        s_wv = stage[1][:, 1280:1536].rearrange("p (k n) -> p k n", k=PAIRS)
        s_wkv = stage[1][0:R, 1536:1792]
        s_weight = stage[1][:, 1792:2304].rearrange("p (k n) -> p k n", k=NF)
        s_disha = stage[1][:, 2304:2560]
        s_c = stage[1][:, 2560:2560 + NF * B].rearrange("p (k b) -> p k b", k=NF)
        s_silu = stage[1][:, 2592:2592 + 3 * NF * B].rearrange("p (j k b) -> p j k b", j=3, k=NF)
        s_wo_t = stage[1][:, 2688:3712].rearrange("p (k n) -> p k n", k=PAIRS)
        s_w_in = probs[:, 0:2, 0:H * R + P]
        w_query, w_latent = s_w_in[:, :, 0:H * R], s_w_in[:, :, H * R:]
        s_gate = [m[0:B, :, :] for m in x_mid]

        def mixed_parts(z, i):
            if not z.has_c and i % 2:
                return [query_m[:, j, :].rearrange("p (k n) -> p k n", k=PAIRS) for j in range(2)]
            return mixed_hi[:, :, :], mixed_lo[:, :, :]

        def normed2(z, g):
            if not z.has_c and g % 2:
                return values[0][:, :, :].rearrange("p k n -> p (k n)").rearrange("p (j d) -> p j d", j=CT)
            return x_norm2[:, :, :]

        wmod_loaded = sem("wmod_loaded")
        qk_loaded = sem("qk_loaded")
        out_weights_loaded = sem("out_weights_loaded")
        c_loaded = sem("c_loaded")
        consts_made = sem("consts_made")
        ident_made = sem("ident_made")
        exp_c_made = sem("exp_c_made")
        silu_steps = sem("silu_steps")
        fold_a = sem("fold_a")
        fold_a_kept = sem("fold_a_kept")
        fold_b = sem("fold_b")
        fold_b_kept = sem("fold_b_kept")
        gate_steps = sem("gate_steps")
        x_loaded = sem("x_loaded")
        x_mid_loaded = [sem(f"x_mid_loaded{i}") for i in range(CHUNKS)]
        gates_loaded = sem("gates_loaded")
        key_row_set = sem("key_row_set")
        query_m_copied = sem("query_m_copied")
        max_row_set = sem("max_row_set")
        out_stored = [sem(f"out_stored{i}") for i in range(CHUNKS)]
        scores_ready = sem("scores_ready")
        exps_done = sem("exps_done")
        max_scores_ready = sem("max_scores_ready")
        maxima_done = sem("maxima_done")
        full = [sem("a_full"), sem("b_full")]
        a_full, b_full = full
        a_drained = sem("a_drained")
        b_drained = sem("b_drained")
        h_hi_done = sem("h_hi_done")
        h_split = sem("h_split")
        w_hi_done = sem("w_hi_done")
        w_split = sem("w_split")
        w_out_hi_done = sem("w_out_hi_done")
        w_out_split = sem("w_out_split")
        mixed_hi_done = sem("mixed_hi_done")
        mixed_split = sem("mixed_split")
        w_ffn_hi_done = sem("w_ffn_hi_done")
        w_ffn_split = sem("w_ffn_split")
        h2_hi_done = sem("h2_hi_done")
        h2_split = sem("h2_split")
        query_hi_done = sem("query_hi_done")
        key_hi_done = sem("key_hi_done")
        adds_done = sem("adds_done")
        heads_done = sem("heads_done")
        heads_kept = sem("heads_kept")
        recips_done = sem("recips_done")
        head_mixed = sem("head_mixed")
        stats1_steps = sem("stats1_steps")
        rstd1_steps = sem("rstd1_steps")
        x_normed = sem("x_normed")
        mod1_set = sem("mod1_set")
        mod2_set = sem("mod2_set")
        gated = sem("gated")
        stats2_steps = sem("stats2_steps")
        rstd2_steps = sem("rstd2_steps")
        x_normed2 = sem("x_normed2")

        block = ctx.enter_context(nc.Block())

        @block.sync
        def _(sp):
            for k in range(NF):
                sp.dma_start(s_c[:, k, :], c[:, k * P:(k + 1) * P].rearrange("b p -> p b"),
                             allow_slow_non_contiguous=True).then_inc(c_loaded, 16)
            sp.dma_start(s_wq, wq.rearrange("(k p) n -> p k n", p=P)).then_inc(qk_loaded, 16)
            sp.dma_start(s_wk, wk_up.rearrange("(k p) n -> p k n", p=P)).then_inc(qk_loaded, 16)
            sp.dma_start(s_wkv, wkv_down).then_inc(qk_loaded, 16)
            sp.dma_start(s_wo, wo.rearrange("(k p) n -> p k n", p=P)).then_inc(qk_loaded, 16)
            x_v = x.rearrange("b (t p) d -> b p t d", p=P)
            sp.dma_start(x_in[:, :, :], x_v[0]).then_inc(x_loaded, 16)
            sp.dma_start(s_wmod, wmod.rearrange("(k p) n -> p k n", p=P)).then_inc(wmod_loaded, 16)
            sp.dma_start(s_wv, wv_up.rearrange("(k p) n -> p k n", p=P)).then_inc(out_weights_loaded, 16)
            sp.dma_start(s_weight, weight.rearrange("(k p) n -> p k n", p=P)).then_inc(out_weights_loaded, 16)
            for k in range(2):
                sp.dma_start(s_disha[k * R:(k + 1) * R, :], disha).then_inc(out_weights_loaded, 16)
            out_v = out.rearrange("b (t p) d -> b p t d", p=P)

            def slot(z):
                for s in range(STEPS):
                    if s == 0 and z.has_n:
                        if not first(z):
                            need_alone(sp, a_full, z.before(0))
                            sp.dma_start(x_in[:, :, :], x_v[value(z.n)]).then_inc(x_loaded, 16)
                        else:
                            sp.wait_ge(gate_steps, 3 + CHUNKS)
                            for g in range(CHUNKS):
                                j, cols = g // 2, slice(g % 2 * P, (g % 2 + 1) * P)
                                sp.dma_start(gates_dram[:, g * P:(g + 1) * P], s_gate[g][:, j, cols]).then_inc(out_stored[g], 16)
                            for g in range(CHUNKS):
                                sp.wait_ge(out_stored[g], 16)
                    if s == 1 and z.has_o:
                        need_alone(sp, b_drained, z.before(1))
                        sp.dma_start(gates[:, :, :].rearrange("p k d -> p (k d)"),
                                     gates_dram[bass.ds(value(z.o), 1), :].partition_broadcast(P)).then_inc(gates_loaded, 16)
                        for g in range(CHUNKS):
                            need_alone(sp, out_stored[g], 16 * (z.o + 1))
                            sp.dma_start(x_mid[g][:, :, :], x_v[value(z.o)][:, g * CT:(g + 1) * CT, :]).then_inc(x_mid_loaded[g], 16)
                    if z.has_n and s == step_of("latent", 1) + 2:
                        need_alone(sp, b_drained, z.through(1, "latent", 1) + 1)
                        sp.dma_start(key_lo[1 - z.par][P - 1:P, :].bitcast(F32), ones_row[:, :].bitcast(F32)).then_inc(key_row_set, 16)
                    for j in range(H):
                        copy, row = STEPS + NT * (j - 1) + 1, step_of("max_row", j) + 1
                        late = row >= STEPS
                        b, there = (z.c, z.has_c) if late else (z.n, z.has_n)
                        if s == copy % STEPS and there:
                            need_alone(sp, scores_ready, 2 * NT * (H * b + j - 1))
                            if j == 0:
                                need_alone(sp, b_drained, z.through(1, "query", 1) + 1)
                            elif j == 6:
                                need_alone(sp, b_drained, z.through(1, "query", 7) + 1)
                            elif j in (2, 4):
                                need_alone(sp, b_drained, z.before(1))
                            sp.dma_start(query_m[:, j % 2, :].bitcast(F32), query[:, j, :].bitcast(F32)).then_inc(query_m_copied, 16)
                        if s == row % STEPS and there:
                            need_alone(sp, a_drained, z.through(0, "max_row", j) + 1)
                            need_alone(sp, query_m_copied, 16 * (H * b + j + 1))
                            need_alone(sp, max_row_set, 16 * (H * b + j))
                            sp.dma_start(query_m[P - 1:P, j % 2, :].bitcast(F32),
                                         max_row[j % 2][:, :].bitcast(F32)).then_inc(max_row_set, 16)
                    for g in range(CHUNKS):
                        if z.has_o and s == z.step("ffn", g) + 1:
                            need_alone(sp, b_drained, z.through(1, "ffn", g) + 1)
                            sp.dma_start(out_v[value(z.o)][:, g * CT:(g + 1) * CT, :], x_mid[g][:, :, :]).then_inc(out_stored[g], 16)

            run_slots(sp, slot)
            for g in range(CHUNKS):
                sp.wait_ge(out_stored[g], 16 * (B + 1))

        @block.tensor
        def _(pe):
            pe.wait_ge(consts_made, 3)
            pe.wait_ge(ident_made, 1)
            pe.wait_ge(qk_loaded, 64)
            fold_out = [ps_score[0], ps_score[1], ps_mix[0], ps_mix[1]]
            for f in range(NF):
                for h in range(H):
                    rows = slice((h % 2) * HD, (h % 2) * HD + HD)
                    last = nc.tensor.matmul(fold_out[2 * f + h % 2][:, (h // 2) * R:(h // 2 + 1) * R],
                                            s_wq[rows, h // 2, f * P:(f + 1) * P], s_wk[rows, h // 2, :],
                                            start=True, stop=True)
            for k in range(NF):
                for p in range(PAIRS):
                    nc.tensor.transpose(ps_max[:, k * HALF + p * P:k * HALF + (p + 1) * P],
                                        s_wo[:, k, p * P:(p + 1) * P], ident[:, :])
            for f in range(NF):
                last = nc.tensor.transpose(ps_a[:, f * R:(f + 1) * R], s_wkv[:, f * P:(f + 1) * P], ident[0:R, 0:R])
            last.then_inc(fold_a, 1)
            pe.wait_ge(wmod_loaded, 16)
            pe.wait_ge(silu_steps, 3)
            for j, part in enumerate((2, 5)):
                for k in range(NF):
                    last = nc.tensor.matmul(ps_b[0:B, j * D:(j + 1) * D], s_silu[:, 2, k, :],
                                            s_wmod[:, k, part * D:(part + 1) * D], start=(k == 0), stop=(k == NF - 1))
            last.then_inc(fold_a, 1)
            pe.wait_ge(fold_a_kept, 9)
            pe.wait_ge(out_weights_loaded, 64)
            for h in range(H):
                rows = slice((h % 2) * HD, (h % 2) * HD + HD)
                bank = fold_out[2 * (h % 2) + h // 4]
                p = h // 2
                nc.tensor.matmul(bank[(h % 2) * R:(h % 2) * R + R, (p % 2) * D:(p % 2 + 1) * D],
                                 s_wv[rows, p, :], s_wo_t[rows, p, :], start=True, stop=True)
            for k in range(NF):
                for o in range(NF):
                    nc.tensor.transpose(ps_max[:, k * HALF + o * P:k * HALF + (o + 1) * P],
                                        s_weight[:, o, k * P:(k + 1) * P], ident[:, :])
            for j, part in enumerate((1, 0, 4, 3)):
                for f in range(NF):
                    for k in range(NF):
                        last = nc.tensor.matmul(ps_a[:, (2 * j + f) * B:(2 * j + f + 1) * B],
                                                s_wmod[:, k, part * D + f * P:part * D + (f + 1) * P],
                                                s_silu[:, 2, k, :], start=(k == 0), stop=(k == NF - 1))
            last.then_inc(fold_b, 1)
            pe.wait_ge(fold_b_kept, 10)
            pe.wait_ge(gate_steps, 2)

            def project(side, rows, cols):
                products = [(w, h, f) for f in range(NF) for w, h in ((w_in_hi, h_hi), (w_in_hi, h_lo), (w_in_lo, h_hi))]
                for j, (w, h, f) in enumerate(products):
                    last = nc.tensor.matmul(side[:, :], w[:, f, rows], h[:, f, cols],
                                            start=(j == 0), stop=(j == len(products) - 1))
                return last

            def mix(z, s):
                h, k = divmod(s, NT)
                par = z.par
                if k == 0:
                    need(pe, heads_kept, H * z.c + h - 1)
                for half in range(2):
                    last = nc.tensor.matmul(ps_mix[h % 2][half * R:half * R + R, :], values[par][:, k, :],
                                     probs[:, s % RING, half * HALF:(half + 1) * HALF],
                                     start=(k == 0), stop=(k == NT - 1))
                if k == NT - 1:
                    last.then_inc(heads_done, 1)

            def slot(z):
                for s in range(STEPS):
                    h, k = divmod(s, NT)
                    if z.has_c:
                        if k == 0:
                            need(pe, max_row_set, 16 * (H * z.c + h + 1))
                        if s == 0:
                            need(pe, key_row_set, 16 * (z.c + 1))
                            if isinstance(z.c, int) and z.c == 0:
                                pe.wait_ge(maxima_done, STEPS - MAX_LAG)
                        for half in range(2):
                            cols = slice(half * HALF, (half + 1) * HALF)
                            need(pe, exps_done, 2 * (STEPS * z.c + s) - 1 + half)
                            nc.tensor.matmul(ps_score[half], key_hi[z.par][:, k * P:(k + 1) * P],
                                             query[:, h, cols], start=True, stop=False)
                            nc.tensor.matmul(ps_score[half], key_lo[z.par][:, k * P:(k + 1) * P],
                                             query_m[:, h % 2, cols], start=False, stop=True).then_inc(scores_ready, 1)
                    if s == 0 and z.has_o:
                        if not z.has_c:
                            need(pe, exps_done, 2 * STEPS * z.c)
                        zo = Slot(z.o, 1 - z.par)
                        mix(zo, STEPS - 1)
                    if s > 0 and z.has_c:
                        if s == 1:
                            need(pe, a_drained, values_drained(z))
                        mix(z, s - 1)
                    item = z.max_item(s)
                    if item:
                        b, m = item
                        hm, qt = divmod(m, NT)
                        kpar = (1 - z.par) if s >= MAX_LAG else z.par
                        if m % (2 * NT) == 0:
                            made = ("query", 2 * (hm // 2) + 1)
                            here = made in [p[2:4] for p in z.lists[1] if (p[4] == 0) == (s < MAX_LAG)]
                            need(pe, b_drained, z.through(1, *made) + 1 if here else z.before(1))
                        need(pe, maxima_done, STEPS * b + m - (0 if z.has_c else 1))
                        bank = z.max_bank(m, ps_max, ps_scores)
                        for half in range(2):
                            last = nc.tensor.matmul(bank[:, half * HALF:(half + 1) * HALF],
                                                    query[:, hm, qt * P:(qt + 1) * P],
                                                    key_hi[kpar][:, half * HALF:(half + 1) * HALF],
                                                    start=True, stop=True)
                        last.then_inc(max_scores_ready, 1)
                    for kind, i, bank, b, w in z.at(s):
                        count = z.through(bank, kind, i)
                        side = ps_side[bank]
                        if kind == "norm_t":
                            half, f = divmod(i, NF)
                            t0 = half * NT // 2
                            if f == 0:
                                need(pe, x_normed, NT * b + t0 + NT // 2)
                            need(pe, a_drained, count)
                            for t in range(4):
                                last = nc.tensor.transpose(side[:, t * P:(t + 1) * P],
                                                           x_in[:, t0 + t, f * P:(f + 1) * P], ident[:, :])
                        elif kind == "latent":
                            need(pe, h_split, 2 * NF * b + NF * (i + 1))
                            if first(z):
                                pe.wait_ge(w_split, 1)
                            need(pe, b_drained, count)
                            last = project(side, slice(H * R, H * R + P), slice(i * HALF, (i + 1) * HALF))
                        elif kind == "values_t":
                            if i == 0:
                                need(pe, key_hi_done, 4 * (b + 1))
                            need(pe, a_drained, count)
                            for t in range(4):
                                last = nc.tensor.transpose(side[:, t * P:(t + 1) * P],
                                                           latent_t[:, (4 * i + t) * P:(4 * i + t + 1) * P], ident[:, :])
                        elif kind == "query":
                            need(pe, b_drained, count)
                            p, half = divmod(i, 2)
                            last = project(side, slice(p * P, (p + 1) * P), slice(half * HALF, (half + 1) * HALF))
                        elif kind == "max_row":
                            need(pe, maxima_done, STEPS * b + NT * (i + 1))
                            need(pe, a_drained, count)
                            last = nc.tensor.matmul(side[0:NT, 0:P], neg_max[:, NT * i:NT * (i + 1)], ident[:, :],
                                                    start=True, stop=True)
                        elif kind == "denominator":
                            need(pe, adds_done, ADDS * (H * b + i + 1))
                            need(pe, a_drained, count)
                            for q in range(QUARTERS):
                                last = nc.tensor.matmul(side[q * QP:(q + 1) * QP, 0:QW], ones_cols[:, :],
                                                        prob_sum[i % 2][:, q * QW:(q + 1) * QW], start=True, stop=True)
                        elif kind == "out_proj":
                            if i == 0:
                                need(pe, w_out_split, b + 1)
                            need(pe, mixed_split, CHUNKS * b + i + 1)
                            need(pe, b_drained, count)
                            m_hi, m_lo = mixed_parts(z, i)
                            products = [(mp, wp, p) for p in range(PAIRS)
                                        for mp, wp in ((m_hi, w_out_hi), (m_lo, w_out_hi), (m_hi, w_out_lo))]
                            for j in range(CT):
                                for q, (mp, wp, p) in enumerate(products):
                                    last = nc.tensor.matmul(side[:, j * D:(j + 1) * D], mp[:, p, j * P:(j + 1) * P],
                                                            wp[:, p, :], start=(q == 0), stop=(q == len(products) - 1))
                        elif kind == "norm2_t":
                            need(pe, x_normed2, NT * b + CT * (i + 1))
                            need(pe, a_drained, count)
                            for f in range(NF):
                                for j in range(CT):
                                    last = nc.tensor.transpose(side[:, (f * CT + j) * P:(f * CT + j + 1) * P],
                                                               normed2(z, i)[:, j, f * P:(f + 1) * P], ident[:, :])
                        elif kind == "ffn":
                            need(pe, h2_split, CHUNKS * b + i + 1)
                            if i == 0:
                                need(pe, w_ffn_split, b + 1)
                            need(pe, b_drained, count)
                            products = [(hp, wp, f) for f in range(NF)
                                        for hp, wp in ((h2_hi, w_ffn_hi), (h2_lo, w_ffn_hi), (h2_hi, w_ffn_lo))]
                            for j in range(CT):
                                for q, (hp, wp, f) in enumerate(products):
                                    last = nc.tensor.matmul(side[:, j * D:(j + 1) * D], hp[:, f, j * P:(j + 1) * P],
                                                            wp[:, f, :], start=(q == 0), stop=(q == len(products) - 1))
                        last.then_inc(full[bank], 1)

            def values_drained(z):
                before = flagged(z.c - 1) if isinstance(z.c, int) else Slot(z.c - 1, 1 - z.par)
                if not isinstance(z.c, int):
                    names = [(kind, i) for (_, _, kind, i, _) in before.lists[0]]
                    return z.before(0) - (len(names) - names.index(("values_t", 1)) - 1)
                return before.through(0, "values_t", 1) + 1

            run_slots(pe, slot)

        @block.scalar
        def _(act):
            act.wait_ge(c_loaded, 32)
            nc.scalar.activation(s_silu[:, 0, :, :], s_c, ACT.Exp, scale=-1.0).then_inc(exp_c_made, 1)

            def split_h2(z, g):
                need(act, a_drained, z.through(0, "norm2_t", g) + 1)
                need(act, b_full, z.through(1, "ffn", g - 1) + 1 if g else z.before(1))
                nc.scalar.activation(h2_hi[:, :, :], h2_t[:, :, :], ACT.Copy).then_inc(h2_hi_done, 1)

            act.wait_ge(fold_a_kept, 8)
            nc.scalar.activation(w_in_hi[:, :, :], s_w_in, ACT.Copy).then_inc(w_hi_done, 1)

            def slot(z):
                for s in range(STEPS):
                    h, k = divmod(s, NT)
                    if z.has_c:
                        old = s - RING
                        ho, ko = divmod(old, NT)
                        need(act, adds_done, ADDS * (H * z.c + ho) + max(ko, 1))
                        for half in range(2):
                            need(act, scores_ready, 2 * (STEPS * z.c + s) + half + 1)
                            nc.scalar.activation(probs[:, s % RING, half * HALF:(half + 1) * HALF], ps_score[half],
                                                 ACT.Exp, scale=SCALE).then_inc(exps_done, 1)
                    if k == 0 and (z.has_c if h else z.has_o):
                        head, bank_of = (H * z.c + h - 1, (h - 1) % 2) if h else (H * z.o + H - 1, 1)
                        need(act, heads_done, head + 1)
                        need(act, head_mixed, 2 * head)
                        nc.scalar.activation(mixed_raw[:, :], ps_mix[bank_of][:, :], ACT.Copy).then_inc(heads_kept, 1)
                    if s == GATE_STEPS[1][z.has_c] and z.has_o:
                        need(act, gated, 2 * (z.o + 1))
                        nc.scalar.activation(w_out_hi[:, :, :], w_out_gated[:, :, :], ACT.Copy).then_inc(w_out_hi_done, 1)
                        nc.scalar.activation(w_ffn_hi[:, :, :], w_ffn_gated, ACT.Copy).then_inc(w_ffn_hi_done, 1)
                    for g in range(CHUNKS):
                        if z.has_o and z.has_c and s == z.step("h2_split", g):
                            split_h2(z, g)
                    for g in range(CHUNKS):
                        if z.has_o and s == z.step("mixed_hi", g):
                            if g == 0:
                                need(act, head_mixed, 2 * H * (z.o + 1))
                            old = g - 1 if z.has_c else g - 2
                            need(act, b_full, z.through(1, "out_proj", old) + 1 if old >= 0 else z.before(1))
                            nc.scalar.activation(mixed_parts(z, g)[0], mixed[1 - z.par][:, :, g * CT * P:(g + 1) * CT * P],
                                                 ACT.Copy).then_inc(mixed_hi_done, 1)
                    for kind, i, bank, b, w in z.at(s):
                        count = z.through(bank, kind, i)
                        if kind == "query":
                            need(act, b_full, count + 1)
                            p, half = divmod(i, 2)
                            for j in range(2):
                                nc.scalar.activation(query[0:R, 2 * p + j, half * HALF:(half + 1) * HALF],
                                                     ps_b[j * R:(j + 1) * R, :], ACT.Copy).then_inc(query_hi_done, 1)
                        elif kind == "latent":
                            need(act, b_full, count + 1)
                            cols = slice(i * HALF, (i + 1) * HALF)
                            nc.scalar.activation(key_hi[1 - z.par][:, cols], ps_b[:, :], ACT.Copy).then_inc(key_hi_done, 1)
                            nc.scalar.activation(latent_t[:, cols], ps_b[:, :], ACT.Copy).then_inc(key_hi_done, 1)
                        elif kind == "norm_t":
                            if i == 0:
                                need(act, mod1_set, b + 1)
                            need(act, a_full, count + 1)
                            half, f = divmod(i, NF)
                            need(act, h_split, 2 * NF * b + i - 1)
                            cols = slice(half * HALF, (half + 1) * HALF)
                            for part, done in ((h_hi[:, f, cols], h_hi_done), (h_whole[:, i % 2, :], a_drained)):
                                nc.scalar.activation(part, ps_a[:, :], ACT.Identity,
                                                     scale=mod1[:, f:f + 1], bias=mod1[:, NF + f:NF + f + 1]).then_inc(done, 1)
                        elif kind == "values_t":
                            need(act, a_full, count + 1)
                            nc.scalar.activation(values[1 - z.par][:, 4 * i:4 * i + 4, :],
                                                 ps_a[:, :].rearrange("p (t n) -> p t n", t=4)[:, :, 0:R],
                                                 ACT.Copy).then_inc(a_drained, 1)
                        elif kind == "denominator":
                            need(act, a_full, count + 1)
                            need(act, head_mixed, 2 * (H * b + i))
                            nc.scalar.activation(prob_total[:, :], ps_a[:, 0:QW], ACT.Copy).then_inc(a_drained, 1)
                        elif kind == "norm2_t":
                            if i == 0:
                                need(act, mod2_set, b + 1)
                            need(act, a_full, count + 1)
                            for f in range(NF):
                                last = nc.scalar.activation(h2_t[:, f, :], ps_a[:, f * CT * P:(f + 1) * CT * P], ACT.Identity,
                                                            scale=mod2[:, f:f + 1], bias=mod2[:, NF + f:NF + f + 1])
                            last.then_inc(a_drained, 1)
                            if not z.has_c:
                                split_h2(z, i)
                        elif kind == "max_row":
                            need(act, a_full, count + 1)
                            need(act, max_row_set, 16 * (H * b + i - 1))
                            nc.scalar.activation(max_row[i % 2][:, :], ps_a[0:NT, 0:P], ACT.Copy).then_inc(a_drained, 1)

            run_slots(act, slot)

        @block.gpsimd
        def _(pool):
            nc.gpsimd.memset(ident[:, :], 0.0).then_inc(consts_made, 1)
            pool.wait_ge(consts_made, 1)
            nc.gpsimd.affine_select(out=ident[:, :], in_=ident[:, :], compare_op=ALU.not_equal, fill=1.0, base=0,
                                    pattern=[[-1, P]], channel_multiplier=1).then_inc(ident_made, 1)
            nc.gpsimd.memset(ones_cols[:, :], 1.0).then_inc(consts_made, 1)
            nc.gpsimd.memset(minus_half[:, :], -0.5).then_inc(consts_made, 1)
            nc.gpsimd.memset(ones_row[:, :].bitcast(F32), 1.0).then_inc(consts_made, 1)

            def inverse_root(moments, rstd, steps, count):
                nc.gpsimd.tensor_scalar(rstd[:, 0, :], moments[:, :, 1], EPS, None, ALU.add).then_inc(steps, 1)
                nc.gpsimd.tensor_scalar(rstd[:, 2, :], moments[:, :, 0], -1.0, None, ALU.mult).then_inc(steps, 1)
                need(pool, steps, count + 2)
                n = rstd.shape[2]
                nc.gpsimd.tensor_tensor(out=rstd[:, 1, :], in0=rstd[:, 0, :], in1=minus_half[:, 0:n], op=ALU.pow).then_inc(steps, 1)
                need_alone(pool, steps, count + 3)

            def add_probs(z, s):
                h, k = divmod(s, NT)
                if k == 0:
                    return
                done = ADDS * (H * z.c + h) + k - 1
                total = prob_sum[h % 2]
                need(pool, exps_done, 2 * (STEPS * z.c + s + 1))
                if k > 1:
                    need(pool, adds_done, done)
                before = probs[:, (s - 1) % RING, :] if k == 1 else total[:, :]
                nc.gpsimd.tensor_tensor(out=total[:, :], in0=before, in1=probs[:, s % RING, :], op=ALU.add).then_inc(adds_done, 1)

            def slot(z):
                for s in range(STEPS):
                    if s == 0 and z.has_o:
                        add_probs(Slot(z.o, 1 - z.par), STEPS - 1)
                    if s > 0 and z.has_c:
                        add_probs(z, s - 1)
                    if s == 0:
                        if z.has_o:
                            need(pool, a_drained, z.before(0))
                            nc.gpsimd.tensor_copy(mod2[:, :], mod_cols[:, bass.ds(value(z.o), 1), 4:8].rearrange("p b k -> p (b k)")).then_inc(mod2_set, 1)
                    if s in APPLY_STEPS and z.has_n:
                        half = APPLY_STEPS.index(s)
                        tiles = slice(half * NT // 2, (half + 1) * NT // 2)
                        need_alone(pool, stats1_steps, 2 * NT * z.n + NT * (half + 1))
                        inverse_root(moments1[:, tiles, :], rstd1[:, :, tiles], rstd1_steps, 3 * (2 * z.n + half))
                        for t in range(NT)[tiles]:
                            nc.gpsimd.tensor_scalar(x_in[:, t, :], x_in[:, t, :], rstd1[:, 2, t:t + 1], rstd1[:, 1, t:t + 1],
                                                    ALU.add, ALU.mult).then_inc(x_normed, 1)
                    if s == APPLY_STEPS[-1] and z.has_n:
                        need(pool, a_drained, z.before(0))
                        if first(z):
                            pool.wait_ge(fold_b_kept, 10)
                        nc.gpsimd.tensor_copy(mod1[:, :], mod_cols[:, bass.ds(value(z.n), 1), 0:4].rearrange("p b k -> p (b k)")).then_inc(mod1_set, 1)
                    if s == GATE_STEPS[0][z.has_c] and z.has_o:
                        need(pool, gates_loaded, 16 * (z.o + 1))
                        need(pool, b_full, z.before(1))
                        nc.gpsimd.tensor_tensor(out=w_out_gated[:, :, :], in0=w_out[:, :, :],
                                                in1=gates[:, 0:1, :].broadcast_to([P, PAIRS, D]), op=ALU.mult).then_inc(gated, 1)
                        nc.gpsimd.tensor_tensor(out=w_ffn_gated[:, :, :], in0=w_ffn[:, :, :],
                                                in1=gates[:, 1:2, :].broadcast_to([P, NF, D]), op=ALU.mult).then_inc(gated, 1)
                    for g in range(CHUNKS):
                        if z.has_o and s == z.step("out_proj", g) + 2:
                            need_alone(pool, stats2_steps, 2 * (NT * z.o + CT * (g + 1)))
                            inverse_root(moments2[g % 2], rstd2[g % 2], rstd2_steps, 3 * (CHUNKS * z.o + g))
                            for j in range(CT):
                                nc.gpsimd.tensor_scalar(normed2(z, g)[:, j, :], x_mid[g][:, j, :], rstd2[g % 2][:, 2, j:j + 1],
                                                        rstd2[g % 2][:, 1, j:j + 1], ALU.add, ALU.mult).then_inc(x_normed2, 1)

            run_slots(pool, slot)

        @block.vector
        def _(dve):
            def statistics(n, t):
                if t == 0:
                    need(dve, x_loaded, 16 * (n + 1))
                nc.vector.bn_stats(stats1[:, t, :], x_in[:, t, :]).then_inc(stats1_steps, 1)
                need_alone(dve, stats1_steps, 2 * (NT * n + t) + 1)
                nc.vector.bn_aggr(moments1[:, t, :], stats1[:, t, :]).then_inc(stats1_steps, 1)

            dve.wait_ge(exp_c_made, 1)
            nc.vector.tensor_scalar(s_silu[:, 1, :, :], s_silu[:, 0, :, :], 1.0, None, ALU.add).then_inc(silu_steps, 1)
            dve.wait_ge(silu_steps, 1)
            nc.vector.reciprocal(s_silu[:, 0, :, :], s_silu[:, 1, :, :]).then_inc(silu_steps, 1)
            dve.wait_ge(silu_steps, 2)
            nc.vector.tensor_tensor(s_silu[:, 2, :, :], s_silu[:, 0, :, :], s_c, ALU.mult).then_inc(silu_steps, 1)
            for t in range(NT):
                statistics(0, t)
            dve.wait_ge(fold_a, 1)
            fold_out = [ps_score[0], ps_score[1], ps_mix[0], ps_mix[1]]
            for f in range(NF):
                for j in range(2):
                    nc.vector.tensor_copy(w_query[:, f, :].rearrange("p (k j n) -> p k j n", k=PAIRS, j=2)[:, :, j, :],
                                          fold_out[2 * f + j][:, 0:PAIRS * R].rearrange("p (k n) -> p k n", k=PAIRS)).then_inc(fold_a_kept, 1)
            for k in range(NF):
                nc.vector.tensor_copy(s_wo_t[:, :, k * P:(k + 1) * P],
                                      ps_max[:, k * HALF:(k + 1) * HALF].rearrange("p (q n) -> p q n", q=PAIRS)).then_inc(fold_a_kept, 1)
            for j in range(2):
                nc.vector.tensor_copy(w_latent[:, :, j * R:(j + 1) * R],
                                      ps_a[:, 0:NF * R].rearrange("p (f n) -> p f n", f=NF)).then_inc(fold_a_kept, 1)
            dve.wait_ge(fold_a, 2)
            sign, size = s_gate[0], s_gate[1]
            raw = ps_b[0:B, :].rearrange("p (j n) -> p j n", j=2)
            nc.vector.tensor_scalar(sign, raw, 0.0, 2.0, ALU.is_ge, ALU.mult).then_inc(fold_a_kept, 1)
            dve.wait_ge(fold_a_kept, 9)
            nc.vector.tensor_scalar(sign, sign, -1.0, None, ALU.add).then_inc(gate_steps, 1)
            dve.wait_ge(gate_steps, 1)
            nc.vector.tensor_tensor(size, raw, sign, ALU.mult).then_inc(gate_steps, 1)
            dve.wait_ge(gate_steps, 2)
            nc.vector.tensor_scalar(size, size, GATE_FLOOR, None, ALU.max).then_inc(gate_steps, 1)
            dve.wait_ge(gate_steps, 3)
            for g in range(CHUNKS):
                j, cols = g // 2, slice(g % 2 * P, (g % 2 + 1) * P)
                nc.vector.tensor_tensor(s_gate[g][:, j, cols], size[:, j, cols], sign[:, j, cols], ALU.mult).then_inc(gate_steps, 1)
            dve.wait_ge(fold_b, 1)
            for j in range(2):
                for k in range(2):
                    nc.vector.tensor_copy(w_out[j * R:(j + 1) * R, 2 * k:2 * k + 2, :],
                                          fold_out[2 * j + k][j * R:(j + 1) * R, :].rearrange("p (q n) -> p q n", q=2)).then_inc(fold_b_kept, 1)
            for k in range(NF):
                nc.vector.tensor_tensor(w_ffn[:, k, :], ps_max[:, k * HALF:k * HALF + D], s_disha, ALU.add).then_inc(fold_b_kept, 1)
            cols = ps_a[:, 0:8 * B].rearrange("p (j b) -> p b j", b=B)
            for j in range(2):
                nc.vector.tensor_scalar(mod_cols[:, :, 4 * j:4 * j + 4], cols[:, :, 4 * j:4 * j + 4], 0.0, None, ALU.add).then_inc(fold_b_kept, 1)
            dve.wait_ge(fold_b_kept, 8)
            for j in range(2):
                nc.vector.tensor_scalar(mod_cols[:, :, 4 * j:4 * j + 2], mod_cols[:, :, 4 * j:4 * j + 2], 1.0, None, ALU.add).then_inc(fold_b_kept, 1)

            def divide(z, s):
                for lag in (*range(1, CUTS + 1), *MIX_LAGS):
                    for kind, i, bank, b, w in z.at(s - lag):
                        if kind != "denominator":
                            continue
                        if lag <= CUTS:
                            if lag == 1:
                                need(dve, a_drained, z.through(bank, kind, i) + 1)
                            cols = slice((lag - 1) * QW // CUTS, lag * QW // CUTS)
                            nc.vector.reciprocal(recip[:, cols], prob_total[:, cols]).then_inc(recips_done, 1)
                            continue
                        need(dve, recips_done, CUTS * (H * b + i + 1))
                        need(dve, heads_kept, H * b + i + 1)
                        mpar = z.par if w == 0 else 1 - z.par
                        half = MIX_LAGS.index(lag)
                        for q in (2 * half, 2 * half + 1):
                            for part in range(0, R, QP):
                                row = i % 2 * R + part
                                last = nc.vector.tensor_tensor(
                                    mixed[mpar][row:row + QP, i // 2, q * QW:(q + 1) * QW],
                                    mixed_raw[half * R + part:half * R + part + QP, q % 2 * QW:(q % 2 + 1) * QW],
                                    recip[q * QP:(q + 1) * QP, :], ALU.mult)
                        last.then_inc(head_mixed, 1)

            dve.wait_ge(w_hi_done, 1)
            nc.vector.tensor_tensor(w_in_lo[:, :, :], s_w_in, w_in_hi[:, :, :].bitcast(F32), ALU.subtract).then_inc(w_split, 1)

            def slot(z):
                for s in range(STEPS):
                    item = z.max_item(s)
                    if item:
                        b, m = item
                        need(dve, max_scores_ready, STEPS * b + m + 1)
                        nc.vector.tensor_reduce(neg_max[:, m:m + 1], z.max_bank(m, ps_max, ps_scores)[:, :], AX_X, ALU.max, negate=True).then_inc(maxima_done, 1)
                    divide(z, s)
                    if s == GATE_STEPS[2][z.has_c] and z.has_o:
                        need(dve, w_out_hi_done, z.o + 1)
                        nc.vector.tensor_tensor(w_out_lo[:, :, :], w_out_gated[:, :, :], w_out_hi[:, :, :].bitcast(F32),
                                                ALU.subtract).then_inc(w_out_split, 1)
                        need(dve, w_ffn_hi_done, z.o + 1)
                        nc.vector.tensor_tensor(w_ffn_lo[:, :, :], w_ffn_gated, w_ffn_hi[:, :, :].bitcast(F32),
                                                ALU.subtract).then_inc(w_ffn_split, 1)
                    for g in range(CHUNKS):
                        if z.has_o and s == z.step("mixed_lo", g):
                            need(dve, mixed_hi_done, CHUNKS * z.o + g + 1)
                            hi, lo = mixed_parts(z, g)
                            nc.vector.tensor_tensor(lo, mixed[1 - z.par][:, :, g * CT * P:(g + 1) * CT * P],
                                                    hi.bitcast(F32), ALU.subtract).then_inc(mixed_split, 1)
                    for kind, i, bank, b, w in z.at(s - 1):
                        if kind == "norm_t":
                            need(dve, h_hi_done, 2 * NF * b + i + 1)
                            need(dve, a_drained, z.through(bank, kind, i) + 1)
                            half, f = divmod(i, NF)
                            cols = slice(half * HALF, (half + 1) * HALF)
                            nc.vector.tensor_tensor(h_lo[:, f, cols], h_whole[:, i % 2, :], h_hi[:, f, cols].bitcast(F32),
                                                    ALU.subtract).then_inc(h_split, 1)
                    for t in range(NT):
                        if z.has_n and not first(z) and s == STATS_STEPS[t]:
                            statistics(z.n, t)
                    for g in range(CHUNKS):
                        if z.has_o and s == z.step("h2_split", g):
                            need(dve, h2_hi_done, CHUNKS * z.o + g + 1)
                            nc.vector.tensor_tensor(h2_lo[:, :, :], h2_t[:, :, :], h2_hi[:, :, :].bitcast(F32),
                                                    ALU.subtract).then_inc(h2_split, 1)
                    for kind, i, bank, b, w in z.at(s):
                        if bank == 0:
                            continue
                        count = z.through(bank, kind, i)
                        if kind == "query":
                            need(dve, query_hi_done, 4 * PAIRS * b + 2 * (i + 1))
                            p, half = divmod(i, 2)
                            cols = slice(half * HALF, (half + 1) * HALF)
                            for j in range(2):
                                last = nc.vector.tensor_tensor(query[R:P, 2 * p + j, cols], ps_b[j * R:(j + 1) * R, :],
                                                               query[0:R, 2 * p + j, cols].bitcast(F32), ALU.subtract)
                            last.then_inc(b_drained, 1)
                        elif kind == "latent":
                            need(dve, key_hi_done, 4 * b + 2 * (i + 1))
                            cols = slice(i * HALF, (i + 1) * HALF)
                            nc.vector.tensor_tensor(key_lo[1 - z.par][:, cols], ps_b[:, :],
                                                    key_hi[1 - z.par][:, cols].bitcast(F32), ALU.subtract).then_inc(b_drained, 1)
                        elif kind == "out_proj":
                            need(dve, b_full, count + 1)
                            need(dve, x_mid_loaded[i], 16 * (b + 1))
                            nc.vector.tensor_tensor(x_mid[i][:, :, :], ps_b[:, :].rearrange("p (j d) -> p j d", j=CT),
                                                    x_mid[i][:, :, :], ALU.add).then_inc(b_drained, 1)
                            need(dve, b_drained, count + 1)
                            for j in range(CT):
                                nc.vector.bn_stats(stats2[i % 2][:, j, :], x_mid[i][:, j, :]).then_inc(stats2_steps, 1)
                            need_alone(dve, stats2_steps, 2 * (NT * b + CT * i) + CT)
                            for j in range(CT):
                                nc.vector.bn_aggr(moments2[i % 2][:, j, :], stats2[i % 2][:, j, :]).then_inc(stats2_steps, 1)
                        elif kind == "ffn":
                            need(dve, b_full, count + 1)
                            nc.vector.tensor_tensor(x_mid[i][:, :, :], ps_b[:, :].rearrange("p (j d) -> p j d", j=CT),
                                                    x_mid[i][:, :, :], ALU.add).then_inc(b_drained, 1)

            run_slots(dve, slot)


_INS = ['L0_attn_x', 'L0_attn_Wq', 'L0_attn_Wkv_down', 'L0_attn_Wk_up', 'L0_attn_Wv_up', 'L0_attn_Wo',
        'L0_ffn_weight', 'L0_ffn_disha', 'L0_c', 'L0_wmod']
_OUTS = [((B, T, D), 'float32')]


def kernel(**inputs):
    import numpy as _np
    import concourse.bacc as _bacc
    from concourse import mybir as _mybir
    from concourse.bass_utils import run_bass_kernel_spmd as _run

    nc = _bacc.Bacc("TRN2", target_bir_lowering=False, num_devices=1)
    arrays, args = {}, []
    for name in _INS:
        a = _np.ascontiguousarray(inputs[name])
        arrays[f"in_{name}_dram"] = a
        args.append(nc.dram_tensor(f"in_{name}_dram", a.shape, _mybir.dt.from_np(a.dtype), kind="ExternalInput").ap())
    for i, (shape, dtype) in enumerate(_OUTS):
        dt = _mybir.dt.from_np(_np.dtype(dtype))
        args.append(nc.dram_tensor(f"out_{i}_dram", shape, dt, kind="ExternalOutput").ap())
    adaln_block(nc, *args)
    r = _run(nc, [arrays], core_ids=[0])
    got = tuple(r.results[0][f"out_{i}_dram"] for i in range(len(_OUTS)))
    return got[0]
```
